# Optimizing a Trainium2 kernel written in Bass

```python
import numpy as np
import jax
import jax.numpy as jnp

def _softmax(x, axis=-1):
    return jax.nn.softmax(x, axis=axis)

def _gelu(x):
    return jax.nn.gelu(x, approximate=True)

def _silu(x):
    return jax.nn.silu(x)

def _sigmoid(x):
    return jax.nn.sigmoid(x)

def _layernorm(x, axis=-1, eps=1e-05):
    m = jnp.mean(x, axis=axis, keepdims=True)
    v = jnp.var(x, axis=axis, keepdims=True)
    return (x - m) / jnp.sqrt(v + eps)

def _scatter_add(tgt, idx, src, axis=0):
    return tgt.at[idx].add(src)

def _segment_sum(src, seg, n):
    return jax.ops.segment_sum(src, seg, n)
kernel_name = 'mk_perceiver_d1_seqx_r4_124983'

def setup_inputs(seed: int=0):
    np.random.seed(seed)
    _w = jnp.asarray

    def _rec_inputs():
        import jax
        import jax.numpy as jnp
        _rk = jax.random.key(seed)
        x = 7.22e-05 + 1 * jax.random.normal(jax.random.fold_in(_rk, 1), (4, 256, 256), jnp.float32)
        _lenS = 256 - jax.random.randint(jax.random.fold_in(_rk, 7), (4,), 0, max(1, 256 // 4) + 1, jnp.int32)
        _lenS2 = 4096 - jax.random.randint(jax.random.fold_in(_rk, 8), (4,), 0, max(1, 4096 // 4) + 1, jnp.int32)
        _ctx_1024P = jax.random.normal(jax.random.fold_in(_rk, 11), (4, 16, 256), jnp.float32)
        _ctx_1024c = jax.random.dirichlet(jax.random.fold_in(_rk, 511), 0.3 * jnp.ones((16,), jnp.float32), (4, 4096))
        _ctx_1024t = jnp.einsum('bsk,bkd->bsd', _ctx_1024c, _ctx_1024P)
        _ctx_1024t = _ctx_1024t * jax.lax.rsqrt(jnp.mean(jnp.square(_ctx_1024t)) + 1e-12) * 0.953939
        ctx_1024 = 4.13588e-05 + 0.999923 * (_ctx_1024t + 0.3 * jax.random.normal(jax.random.fold_in(_rk, 611), (4, 4096, 256), jnp.float32))
        return (x, ctx_1024)
    x, ctx_1024 = _rec_inputs()

    def _L0_xattn_setup():
        import jax, jax.numpy as jnp
        import numpy as np
        HEADS = 8
        DIM_HEAD = 64
        key = jax.random.key(seed)
        ks = jax.random.split(key, 9)
        B, N1, N2, D = (4, 512, 512, 256)
        inner = HEADS * DIM_HEAD
        s_in = 1.0 / np.sqrt(D)
        s_inner = 1.0 / np.sqrt(inner)
        return {'x1': jax.random.normal(ks[0], (B, N1, D), jnp.float32), 'x2': jax.random.normal(ks[1], (B, N2, D), jnp.float32), 'Wq1': jax.random.normal(ks[2], (D, inner), jnp.float32) * s_in, 'Wk1': jax.random.normal(ks[3], (D, inner), jnp.float32) * s_in, 'Wv1': jax.random.normal(ks[4], (D, inner), jnp.float32) * s_in, 'Wk2': jax.random.normal(ks[5], (D, inner), jnp.float32) * s_in, 'Wv2': jax.random.normal(ks[6], (D, inner), jnp.float32) * s_in, 'Wo': jax.random.normal(ks[7], (inner, D), jnp.float32) * s_inner, 'bo': jnp.zeros((D,), jnp.float32)}
    _L0_xattn_all = _L0_xattn_setup()
    _L0_xattn_in = {k: v for k, v in _L0_xattn_all.items() if k in ('Wq1', 'Wk1', 'Wv1', 'Wk2', 'Wv2', 'Wo', 'bo')}
    del _L0_xattn_all

    def _L0_attn_setup():
        import jax, jax.numpy as jnp
        import numpy as np
        B, T, D = (4, 256, 256)
        H = 16
        DS, DC, EXP = (16, 4, 2)
        DIN = EXP * D
        DTR = D // 16
        TOPK_RATIO = 0.25
        EPS = 1e-05

        def _attn_core(x, Wq, bq, Wk, bk, Wv, bv, Wo, bo):
            b, L, d = x.shape
            hd = d // H
            q = (x @ Wq + bq).reshape(b, L, H, hd)
            k = (x @ Wk + bk).reshape(b, L, H, hd)
            v = (x @ Wv + bv).reshape(b, L, H, hd)
            scores = jnp.einsum('bqhd,bkhd->bhqk', q, k) / jnp.sqrt(jnp.float32(hd))
            p = jax.nn.softmax(scores, axis=-1)
            o = jnp.einsum('bhqk,bkhd->bqhd', p, v).reshape(b, L, d)
            return o @ Wo + bo

        def _ssm_core(u, in_w, conv_w, conv_b, xproj_w, dt_w, dt_b, A_log, Dp, out_w):
            b, L, _ = u.shape
            xi, z = jnp.split(u @ in_w, 2, axis=-1)
            xp = jnp.pad(xi, ((0, 0), (DC - 1, 0), (0, 0)))
            xc = conv_b + sum((xp[:, j:j + L] * conv_w[:, j] for j in range(DC)))
            xc = jax.nn.silu(xc)
            proj = xc @ xproj_w
            dtp = proj[..., :DTR]
            Bm = proj[..., DTR:DTR + DS]
            Cm = proj[..., DTR + DS:]
            delta = jax.nn.softplus(dtp @ dt_w + dt_b)
            A = -jnp.exp(A_log)
            dA = jnp.exp(delta[..., None] * A)
            dBu = (delta * xc)[..., None] * Bm[:, :, None, :]

            def step(h, inp):
                dA_t, dBu_t, C_t = inp
                h = dA_t * h + dBu_t
                return (h, jnp.einsum('bds,bs->bd', h, C_t))
            xs = (jnp.moveaxis(dA, 1, 0), jnp.moveaxis(dBu, 1, 0), jnp.moveaxis(Cm, 1, 0))
            _, ys = jax.lax.scan(step, jnp.zeros((b, DIN, DS), u.dtype), xs)
            y = jnp.moveaxis(ys, 0, 1) + xc * Dp
            y = y * jax.nn.silu(z)
            return y @ out_w
        key = jax.random.key(seed)
        ks = jax.random.split(key, 16)

        def n(k, shape, scale=0.02):
            return jax.random.normal(k, shape, jnp.float32) * scale
        return {'x': jax.random.normal(ks[0], (B, T, D), jnp.float32), 'ln_w': jnp.ones((D,), jnp.float32), 'ln_b': jnp.zeros((D,), jnp.float32), 'r_w1': n(ks[1], (D, D // 2)), 'r_b1': jnp.zeros((D // 2,), jnp.float32), 'r_w2': n(ks[2], (D // 2, 1)), 'r_b2': jnp.zeros((1,), jnp.float32), 'Wq': n(ks[3], (D, D)), 'bq': jnp.zeros((D,), jnp.float32), 'Wk': n(ks[4], (D, D)), 'bk': jnp.zeros((D,), jnp.float32), 'Wv': n(ks[5], (D, D)), 'bv': jnp.zeros((D,), jnp.float32), 'Wo': n(ks[6], (D, D)), 'bo': jnp.zeros((D,), jnp.float32), 'in_w': n(ks[7], (D, 2 * DIN)), 'conv_w': n(ks[8], (DIN, DC), 0.1), 'conv_b': jnp.zeros((DIN,), jnp.float32), 'xproj_w': n(ks[9], (DIN, DTR + 2 * DS)), 'dt_w': n(ks[10], (DTR, DIN), 0.1), 'dt_b': jnp.full((DIN,), -4.0, jnp.float32) + n(ks[11], (DIN,), 0.1), 'A_log': jnp.log(jnp.broadcast_to(jnp.arange(1, DS + 1, dtype=jnp.float32), (DIN, DS))), 'Dp': jnp.ones((DIN,), jnp.float32), 'out_w': n(ks[12], (DIN, D))}
    _L0_attn_all = _L0_attn_setup()
    _L0_attn_in = {k: v for k, v in _L0_attn_all.items() if k in ('ln_w', 'ln_b', 'r_w1', 'r_b1', 'r_w2', 'r_b2', 'Wq', 'bq', 'Wk', 'bk', 'Wv', 'bv', 'Wo', 'bo', 'in_w', 'conv_w', 'conv_b', 'xproj_w', 'dt_w', 'dt_b', 'A_log', 'Dp', 'out_w')}
    del _L0_attn_all

    def _L0_ffn_setup():
        import jax, jax.numpy as jnp
        import numpy as np
        from jax import lax
        DIM = 256
        HID = 512
        E = 8
        K = 2
        B, T = (2, 128)
        key = jax.random.key(seed)
        ks = jax.random.split(key, 5)
        scale = 1.0 / np.sqrt(DIM)
        x = jax.random.normal(ks[0], (B, T, DIM), dtype=jnp.float32)
        router_w = jax.random.normal(ks[1], (E, DIM), dtype=jnp.float32) * scale
        w_gate = jax.random.normal(ks[2], (E, HID, DIM), dtype=jnp.float32) * scale
        w_up = jax.random.normal(ks[3], (E, HID, DIM), dtype=jnp.float32) * scale
        w_down = jax.random.normal(ks[4], (E, DIM, HID), dtype=jnp.float32) * (1.0 / np.sqrt(HID))
        return {'x': x, 'router_w': router_w, 'w_gate': w_gate, 'w_up': w_up, 'w_down': w_down}
    _L0_ffn_all = _L0_ffn_setup()
    _L0_ffn_in = {k: v for k, v in _L0_ffn_all.items() if k in ('router_w', 'w_gate', 'w_up', 'w_down')}
    del _L0_ffn_all
    return {'x': x, 'ctx_1024': ctx_1024, 'L0_xattn_Wq1': _L0_xattn_in['Wq1'], 'L0_xattn_Wk1': _L0_xattn_in['Wk1'], 'L0_xattn_Wv1': _L0_xattn_in['Wv1'], 'L0_xattn_Wk2': _L0_xattn_in['Wk2'], 'L0_xattn_Wv2': _L0_xattn_in['Wv2'], 'L0_xattn_Wo': _L0_xattn_in['Wo'], 'L0_xattn_bo': _L0_xattn_in['bo'], 'L0_attn_ln_w': _L0_attn_in['ln_w'], 'L0_attn_ln_b': _L0_attn_in['ln_b'], 'L0_attn_r_w1': _L0_attn_in['r_w1'], 'L0_attn_r_b1': _L0_attn_in['r_b1'], 'L0_attn_r_w2': _L0_attn_in['r_w2'], 'L0_attn_r_b2': _L0_attn_in['r_b2'], 'L0_attn_Wq': _L0_attn_in['Wq'], 'L0_attn_bq': _L0_attn_in['bq'], 'L0_attn_Wk': _L0_attn_in['Wk'], 'L0_attn_bk': _L0_attn_in['bk'], 'L0_attn_Wv': _L0_attn_in['Wv'], 'L0_attn_bv': _L0_attn_in['bv'], 'L0_attn_Wo': _L0_attn_in['Wo'], 'L0_attn_bo': _L0_attn_in['bo'], 'L0_attn_in_w': _L0_attn_in['in_w'], 'L0_attn_conv_w': _L0_attn_in['conv_w'], 'L0_attn_conv_b': _L0_attn_in['conv_b'], 'L0_attn_xproj_w': _L0_attn_in['xproj_w'], 'L0_attn_dt_w': _L0_attn_in['dt_w'], 'L0_attn_dt_b': _L0_attn_in['dt_b'], 'L0_attn_A_log': _L0_attn_in['A_log'], 'L0_attn_Dp': _L0_attn_in['Dp'], 'L0_attn_out_w': _L0_attn_in['out_w'], 'L0_ffn_router_w': _L0_ffn_in['router_w'], 'L0_ffn_w_gate': _L0_ffn_in['w_gate'], 'L0_ffn_w_up': _L0_ffn_in['w_up'], 'L0_ffn_w_down': _L0_ffn_in['w_down']}

def reference(x, ctx_1024, L0_xattn_Wq1, L0_xattn_Wk1, L0_xattn_Wv1, L0_xattn_Wk2, L0_xattn_Wv2, L0_xattn_Wo, L0_xattn_bo, L0_attn_ln_w, L0_attn_ln_b, L0_attn_r_w1, L0_attn_r_b1, L0_attn_r_w2, L0_attn_r_b2, L0_attn_Wq, L0_attn_bq, L0_attn_Wk, L0_attn_bk, L0_attn_Wv, L0_attn_bv, L0_attn_Wo, L0_attn_bo, L0_attn_in_w, L0_attn_conv_w, L0_attn_conv_b, L0_attn_xproj_w, L0_attn_dt_w, L0_attn_dt_b, L0_attn_A_log, L0_attn_Dp, L0_attn_out_w, L0_ffn_router_w, L0_ffn_w_gate, L0_ffn_w_up, L0_ffn_w_down):
    import jax
    import jax.numpy as jnp

    def _L0_xattn_ref(x1, x2, Wq1, Wk1, Wv1, Wk2, Wv2, Wo, bo):
        import jax, jax.numpy as jnp
        import numpy as np
        HEADS = 8
        DIM_HEAD = 64
        h, d = (HEADS, DIM_HEAD)
        scale = d ** (-0.5)
        B, N1, _ = x1.shape
        N2 = x2.shape[1]

        def split_heads(t, n):
            return t.reshape(B, n, h, d)
        q1 = split_heads(x1 @ Wq1, N1)
        k1 = split_heads(x1 @ Wk1, N1)
        v1 = split_heads(x1 @ Wv1, N1)
        k2 = split_heads(x2 @ Wk2, N2)
        v2 = split_heads(x2 @ Wv2, N2)
        k = jnp.concatenate([k1, k2], axis=1)
        v = jnp.concatenate([v1, v2], axis=1)
        sim = jnp.einsum('bihd,bjhd->bhij', q1.astype(jnp.float32), k.astype(jnp.float32)) * scale
        attn = jax.nn.softmax(sim, axis=-1)
        out = jnp.einsum('bhij,bjhd->bihd', attn, v)
        out = out.reshape(B, N1, h * d)
        return out @ Wo + bo

    def _L0_attn_ref(x, ln_w, ln_b, r_w1, r_b1, r_w2, r_b2, Wq, bq, Wk, bk, Wv, bv, Wo, bo, in_w, conv_w, conv_b, xproj_w, dt_w, dt_b, A_log, Dp, out_w):
        import jax, jax.numpy as jnp
        import numpy as np
        B, T, D = (4, 256, 256)
        H = 16
        DS, DC, EXP = (16, 4, 2)
        DIN = EXP * D
        DTR = D // 16
        TOPK_RATIO = 0.25
        EPS = 1e-05

        def _attn_core(x, Wq, bq, Wk, bk, Wv, bv, Wo, bo):
            b, L, d = x.shape
            hd = d // H
            q = (x @ Wq + bq).reshape(b, L, H, hd)
            k = (x @ Wk + bk).reshape(b, L, H, hd)
            v = (x @ Wv + bv).reshape(b, L, H, hd)
            scores = jnp.einsum('bqhd,bkhd->bhqk', q, k) / jnp.sqrt(jnp.float32(hd))
            p = jax.nn.softmax(scores, axis=-1)
            o = jnp.einsum('bhqk,bkhd->bqhd', p, v).reshape(b, L, d)
            return o @ Wo + bo

        def _ssm_core(u, in_w, conv_w, conv_b, xproj_w, dt_w, dt_b, A_log, Dp, out_w):
            b, L, _ = u.shape
            xi, z = jnp.split(u @ in_w, 2, axis=-1)
            xp = jnp.pad(xi, ((0, 0), (DC - 1, 0), (0, 0)))
            xc = conv_b + sum((xp[:, j:j + L] * conv_w[:, j] for j in range(DC)))
            xc = jax.nn.silu(xc)
            proj = xc @ xproj_w
            dtp = proj[..., :DTR]
            Bm = proj[..., DTR:DTR + DS]
            Cm = proj[..., DTR + DS:]
            delta = jax.nn.softplus(dtp @ dt_w + dt_b)
            A = -jnp.exp(A_log)
            dA = jnp.exp(delta[..., None] * A)
            dBu = (delta * xc)[..., None] * Bm[:, :, None, :]

            def step(h, inp):
                dA_t, dBu_t, C_t = inp
                h = dA_t * h + dBu_t
                return (h, jnp.einsum('bds,bs->bd', h, C_t))
            xs = (jnp.moveaxis(dA, 1, 0), jnp.moveaxis(dBu, 1, 0), jnp.moveaxis(Cm, 1, 0))
            _, ys = jax.lax.scan(step, jnp.zeros((b, DIN, DS), u.dtype), xs)
            y = jnp.moveaxis(ys, 0, 1) + xc * Dp
            y = y * jax.nn.silu(z)
            return y @ out_w
        b, t, d = x.shape
        k = min(max(1, int(TOPK_RATIO * t)), t)
        mu = x.mean(-1, keepdims=True)
        var = ((x - mu) ** 2).mean(-1, keepdims=True)
        xn = (x - mu) * jax.lax.rsqrt(var + EPS) * ln_w + ln_b
        scores = jnp.squeeze(jax.nn.gelu(xn @ r_w1 + r_b1) @ r_w2 + r_b2, -1)
        _, topk_idx = jax.lax.top_k(scores, k)
        bidx = jnp.arange(b)[:, None]
        mask = jnp.zeros((b, t), bool).at[bidx, topk_idx].set(True)
        order = jnp.argsort(mask.astype(jnp.int32), axis=1)
        bottom_idx = order[:, :t - k]
        x_ssm = xn[bidx, bottom_idx]
        d_ssm_tok = _ssm_core(x_ssm, in_w, conv_w, conv_b, xproj_w, dt_w, dt_b, A_log, Dp, out_w)
        delta_ssm = jnp.zeros_like(xn).at[bidx, bottom_idx].set(d_ssm_tok)
        x_attn = xn[bidx, topk_idx]
        d_attn_tok = _attn_core(x_attn, Wq, bq, Wk, bk, Wv, bv, Wo, bo)
        delta_attn = jnp.zeros_like(xn).at[bidx, topk_idx].set(d_attn_tok)
        delta = jnp.where(mask[..., None], delta_attn, delta_ssm)
        return x + delta

    def _L0_ffn_ref(x, router_w, w_gate, w_up, w_down):
        import jax, jax.numpy as jnp
        import numpy as np
        from jax import lax
        DIM = 256
        HID = 512
        E = 8
        K = 2
        B, T = (2, 128)
        Bb, Tt, D = x.shape
        N = Bb * Tt
        xf = x.reshape(N, D)
        logits = xf @ router_w.T
        routing = jax.nn.softmax(logits, axis=-1)
        top_w, top_i = lax.top_k(routing, K)
        top_w = top_w / jnp.sum(top_w, axis=-1, keepdims=True)
        combine = jnp.zeros((N, E), dtype=x.dtype)
        combine = combine.at[jnp.arange(N)[:, None], top_i].add(top_w)
        g = jnp.einsum('nd,ehd->neh', xf, w_gate)
        u = jnp.einsum('nd,ehd->neh', xf, w_up)
        h = jax.nn.silu(g) * u
        y = jnp.einsum('neh,edh->ned', h, w_down)
        out = jnp.einsum('ned,ne->nd', y, combine)
        return out.reshape(Bb, Tt, D)
    x = x + _L0_xattn_ref(_layernorm(x, axis=-1), ctx_1024, L0_xattn_Wq1, L0_xattn_Wk1, L0_xattn_Wv1, L0_xattn_Wk2, L0_xattn_Wv2, L0_xattn_Wo, L0_xattn_bo)
    x = x + _L0_attn_ref(_layernorm(x, axis=-1), L0_attn_ln_w, L0_attn_ln_b, L0_attn_r_w1, L0_attn_r_b1, L0_attn_r_w2, L0_attn_r_b2, L0_attn_Wq, L0_attn_bq, L0_attn_Wk, L0_attn_bk, L0_attn_Wv, L0_attn_bv, L0_attn_Wo, L0_attn_bo, L0_attn_in_w, L0_attn_conv_w, L0_attn_conv_b, L0_attn_xproj_w, L0_attn_dt_w, L0_attn_dt_b, L0_attn_A_log, L0_attn_Dp, L0_attn_out_w)
    x = x + _L0_ffn_ref(_layernorm(x, axis=-1), L0_ffn_router_w, L0_ffn_w_gate, L0_ffn_w_up, L0_ffn_w_down)
    return x

_drawn_inputs = setup_inputs


def setup_inputs(seed=0):
    import zlib

    import numpy as np

    out = dict(_drawn_inputs(seed))
    spreads = {'L0_xattn_bo': (0.0, 0.1),
     'L0_attn_ln_w': (1.0, 0.2),
     'L0_attn_ln_b': (0.0, 0.1),
     'L0_attn_r_b1': (0.0, 0.1),
     'L0_attn_bq': (0.0, 0.1),
     'L0_attn_bk': (0.0, 0.1),
     'L0_attn_bv': (0.0, 0.1),
     'L0_attn_bo': (0.0, 0.1),
     'L0_attn_conv_b': (0.0, 0.1),
     'L0_attn_Dp': (1.0, 0.2)}
    factors = {}
    for name, (base, spread) in spreads.items():
        noise = np.random.default_rng([zlib.crc32(name.encode()), seed]).standard_normal(out[name].shape)
        drawn = base * np.exp(spread * noise) if base else spread * noise
        out[name] = jnp.asarray(drawn.astype(out[name].dtype))
    for name, factor in factors.items():
        out[name] = (out[name] * factor).astype(out[name].dtype)
    return out
```

```python
from contextlib import ExitStack
import numpy as np
import concourse.bass as bass
from concourse import mybir

F32 = mybir.dt.float32
F32R = mybir.dt.float32r
ALU = mybir.AluOpType
ACT = mybir.ActivationFunctionType
AX_X = mybir.AxisListType.X

P = 128
B, N1, D = 4, 256, 256
N2 = 4096
DC = D // P
QT = N1 // P
TT = B * QT
HEADS, HD = 8, 64
INNER = HEADS * HD
IC = INNER // P
PAIRS = IC
KG = 512
NG = 1 + N2 // KG
KT = (N1 + N2) // P

AH, AHD = 16, 16
TOP = N1 // 4
NS = N1 - TOP
HC = P // AHD
RH = D // 2
DIN = 2 * D
CT = DIN // P
DS, DCONV = 16, 4
DTR = D // 16
RANK = DTR + 2 * DS
GELU = 0.7978845608028654

E, K_TOP, HID = 8, 2, 512
HC2 = HID // P
EPS = 1e-5
OPEN = 1
LAG = 2


def group_keys(g):
    return (0, N1) if g == 0 else (N1 + (g - 1) * KG, KG)


class Norm:

    STEPS = 6

    def __init__(self, sb, sem, name, n):
        self.n = n
        self.stats = sb(f"{name}_stats", [P, n, 6])
        self.agg = sb(f"{name}_agg", [P, n, 2])
        self.var = sb(f"{name}_var", [P, n])
        self.root_var = sb(f"{name}_root_var", [P, n])
        self.guess = sb(f"{name}_guess", [P, n])
        self.square = sb(f"{name}_square", [P, n])
        self.factor = sb(f"{name}_factor", [P, n])
        self.rstd = sb(f"{name}_rstd", [P, n])
        self.done = sem(f"{name}_done")
        self.root_done = sem(f"{name}_root_done")
        self.per_call = 3 * n + self.STEPS

    def normalize(self, dve, calls, x, out):
        n, done = self.n, self.done
        at = calls * self.per_call
        for t in range(n):
            dve.bn_stats(self.stats[:, t, :], x[:, t, :]).then_inc(done, 1)
        dve.wait_ge(done, at + n)
        for t in range(n):
            dve.bn_aggr(self.agg[:, t, :], self.stats[:, t, :]).then_inc(done, 1)
        dve.wait_ge(done, at + 2 * n)
        dve.tensor_scalar(self.var[:, :], self.agg[:, :, 1], EPS, None, ALU.add).then_inc(done, 1)
        dve.wait_ge(self.root_done, calls + 1)
        dve.reciprocal(self.guess[:, :], self.root_var[:, :]).then_inc(done, 1)
        dve.wait_ge(done, at + 2 * n + 2)
        dve.tensor_tensor(self.square[:, :], self.guess[:, :], self.guess[:, :], ALU.mult).then_inc(done, 1)
        dve.wait_ge(done, at + 2 * n + 3)
        dve.scalar_tensor_tensor(self.factor[:, :], self.square[:, :], -0.5, self.var[:, :], ALU.mult,
                                 ALU.mult).then_inc(done, 1)
        dve.wait_ge(done, at + 2 * n + 4)
        dve.scalar_tensor_tensor(self.rstd[:, :], self.factor[:, :], 1.5, self.guess[:, :], ALU.add,
                                 ALU.mult).then_inc(done, 2)
        dve.wait_ge(done, at + 2 * n + 6)
        for t in range(n):
            dve.tensor_scalar(out[:, t, :], x[:, t, :], self.agg[:, t, 0:1], self.rstd[:, t:t + 1],
                              ALU.subtract, ALU.mult).then_inc(done, 1)

    def root(self, act, calls):
        act.wait_ge(self.done, calls * self.per_call + 2 * self.n + 1)
        act.activation(self.root_var[:, :], self.var[:, :], ACT.Sqrt).then_inc(self.root_done, 1)

    def tiles_done(self, calls, tiles):
        return calls * self.per_call + 2 * self.n + self.STEPS + tiles


def cross_attention(nc, x, ctxT, w, X1, ident, banks):
    wq, wk1, wv1, wk2, wv2, wo, bo = (w[n] for n in ("Wq1", "Wk1", "Wv1", "Wk2", "Wv2", "Wo", "bo"))
    ctx = ExitStack()
    with ctx:
        def sb(name, shape, dt=F32):
            return ctx.enter_context(nc.sbuf_tensor(name, shape, dt))

        def sem(name):
            return ctx.enter_context(nc.semaphore(name))

        ones = sb("xa_ones", [P, P], F32R)
        one = sb("xa_one", [P, 1])
        ctx_raw = sb("xa_ctx_raw", [P, 2, DC, KG])
        ctx_hi = sb("xa_ctx_hi", [P, DC, N2], F32R)
        ctx_lo = sb("xa_ctx_lo", [P, DC, N2], F32R)
        xl_T = sb("xa_xl_T", [P, DC, B * N1])
        own_hi = sb("xa_own_hi", [P, DC, N1], F32R)
        own_lo = sb("xa_own_lo", [P, DC, N1], F32R)
        w_raw = sb("xa_w_raw", [P, 5, DC, P])
        w_hi = sb("xa_w_hi", [P, 4, DC, P], F32R)
        w_lo = sb("xa_w_lo", [P, 4, DC, P], F32R)
        q_w_hi = sb("xa_q_w_hi", [P, DC, 2, 2, HD], F32R)
        q_w_lo = sb("xa_q_w_lo", [P, DC, 2, 2, HD], F32R)
        q_hi = sb("xa_q_hi", [P, 2, N1], F32R)
        q_lo = sb("xa_q_lo", [P, 2, N1], F32R)
        keys = [sb(f"xa_keys{h}", [P, KT * P], F32R) for h in range(2)]
        vals = sb("xa_vals", [P, KT, 2, HD + 1])
        maxes = sb("xa_maxes", [P, 4, NG])
        rowmax = sb("xa_rowmax", [P, 4])
        neg_diag = sb("xa_neg_diag", [P, 2, N1], F32R)
        probs = sb("xa_probs", [P, 4, 2 * N1])
        rsum = sb("xa_rsum", [P, 4])
        heads_out = sb("xa_heads_out", [P, QT, INNER])
        heads_T = sb("xa_heads_T", [P, QT, IC, P])
        wo_sb = sb("xa_wo", [P, IC, D])
        bo_sb = sb("xa_bo", [P, D])
        xl = probs[:, :, :].rearrange("p a n -> p (a n)").rearrange("p (t d) -> p t d", d=D)

        x_loaded = sem("xa_x_loaded")
        norm = Norm(sb, sem, "xa_norm", TT)
        setup = sem("xa_setup")
        ident_ready = sem("xa_ident_ready")
        xl_transposed = sem("xa_xl_transposed")
        xl_T_stored = sem("xa_xl_T_stored")
        own_hi_done = sem("xa_own_hi_done")
        own_split = sem("xa_own_split")
        ctx_loaded = [sem(f"xa_ctx_loaded{i}") for i in range(2)]
        ctx_hi_done = sem("xa_ctx_hi_done")
        ctx_split = sem("xa_ctx_split")
        w_loaded = sem("xa_w_loaded")
        w_hi_done = sem("xa_w_hi_done")
        w_split = sem("xa_w_split")
        q_projected = sem("xa_q_projected")
        q_hi_done = sem("xa_q_hi_done")
        q_split = sem("xa_q_split")
        k_projected = sem("xa_k_projected")
        k_hi_done = sem("xa_k_hi_done")
        k_split = sem("xa_k_split")
        v_projected = sem("xa_v_projected")
        v_stored = sem("xa_v_stored")
        max_scored = sem("xa_max_scored")
        max_reduced = sem("xa_max_reduced")
        rowmax_done = sem("xa_rowmax_done")
        diag_ready = sem("xa_diag_ready")
        scores_ready = sem("xa_scores_ready")
        exp_done = sem("xa_exp_done")
        pv_done = sem("xa_pv_done")
        rsum_done = sem("xa_rsum_done")
        o_normalized = sem("xa_o_normalized")
        o_transposed = sem("xa_o_transposed")
        heads_T_done = sem("xa_heads_T_done")
        out_projected = sem("xa_out_projected")
        x1_done = sem("xa_x1_done")

        k_bank = banks[0:2]
        s_bank = banks[2:6]
        v_bank = banks[6:8]

        block = ctx.enter_context(nc.Block())

        @block.sync
        def _(sp):
            sp.dma_start(X1[:, :, :], x.rearrange("b (t p) d -> p (b t) d", p=P)).then_inc(x_loaded, 16)
            sp.dma_start(bo_sb[:, :], bo.rearrange("(a d) -> a d", a=1).broadcast_to([P, D])).then_inc(x_loaded, 16)
            sp.dma_start(wo_sb[:, :, :], wo.rearrange("(c p) n -> p c n", p=P)).then_inc(x_loaded, 16)

            def load_pair(pair):
                for kind, w in enumerate((wq, wk1, wk2, wv1, wv2)):
                    sp.dma_start(w_raw[:, kind, :, :],
                                 w.rearrange("(c p) n -> p c n", p=P)[:, :, bass.ds(pair * P, P)]
                                 ).then_inc(w_loaded, 16)

            load_pair(0)
            with sp.Fori(0, B) as b:
                for c in range(N2 // KG):
                    if c < 2:
                        sp.wait_ge(ctx_split, b * (N2 // KG) + OPEN)
                    else:
                        sp.wait_ge(ctx_split, b * (N2 // KG) + c - 1 + OPEN)
                    sp.dma_start(ctx_raw[:, c % 2, :, :],
                                 ctxT[bass.ds(b, 1), :, c * KG:(c + 1) * KG].rearrange(
                                     "o (c p) n -> p (o c) n", p=P)).then_inc(ctx_loaded[c % 2], 16)
                with sp.Fori(0, PAIRS) as p:
                    sp.wait_ge(w_split, (b * PAIRS + p) * 3 + 3)
                    load_pair((p + 1) % PAIRS)
            sp.wait_ge(w_loaded, 5 * 16 * (B * PAIRS + 1))

        @block.gpsimd
        def _(pool):
            pool.sem_inc(ctx_split, OPEN)
            pool.memset(ident[:, :], 0.0).then_inc(setup, 1)
            pool.memset(ones[:, :].bitcast(F32), 1.0).then_inc(setup, 1)
            pool.memset(vals[:, :, :, HD:HD + 1], 1.0).then_inc(setup, 1)
            pool.memset(one[:, :], 1.0).then_inc(setup, 1)
            pool.wait_ge(setup, 4)
            pool.affine_select(out=ident[:, :], in_=ident[:, :], compare_op=ALU.not_equal, fill=1.0,
                               base=0, pattern=[[-1, P]], channel_multiplier=1).then_inc(ident_ready, 1)

            def split_pair(done):
                pool.wait_ge(w_loaded, 5 * 16 * (done + 1))
                kv_raw = w_raw[:, 1:5, :, :]
                q_raw = w_raw[:, 0, :, :].rearrange("p c (h e) -> p c h e", h=2)
                pool.tensor_tensor(w_hi[:, :, :, :], kv_raw, kv_one, ALU.mult).then_inc(w_hi_done, 1)
                for dup in range(2):
                    pool.tensor_tensor(q_w_hi[:, :, :, dup, :], q_raw, q_one, ALU.mult).then_inc(w_hi_done, 1)
                pool.wait_ge(w_hi_done, 3 * (done + 1))
                pool.tensor_tensor(w_lo[:, :, :, :], kv_raw, w_hi[:, :, :, :].bitcast(F32),
                                   ALU.subtract).then_inc(w_split, 1)
                for dup in range(2):
                    pool.tensor_tensor(q_w_lo[:, :, :, dup, :], q_raw, q_w_hi[:, :, :, dup, :].bitcast(F32),
                                       ALU.subtract).then_inc(w_split, 1)

            ctx_one = one[:, :].unsqueeze(2).broadcast_to([P, DC, KG])
            kv_one = one[:, :].unsqueeze(2).unsqueeze(3).broadcast_to([P, 4, DC, P])
            q_one = one[:, :].unsqueeze(2).unsqueeze(3).broadcast_to([P, DC, 2, HD])
            split_pair(0)
            pool.wait_ge(xl_T_stored, TT)
            with pool.Fori(0, B) as b:
                pool.wait_ge(v_projected, b * (PAIRS * NG) + OPEN)
                for c in range(N2 // KG):
                    at = slice(c * KG, (c + 1) * KG)
                    pool.wait_ge(ctx_loaded[c % 2], b * (16 * N2 // KG // 2) + 16 * (c // 2 + 1))
                    raw = ctx_raw[:, c % 2, :, :]
                    pool.tensor_tensor(ctx_hi[:, :, at], raw, ctx_one, ALU.mult).then_inc(ctx_hi_done, 1)
                    pool.wait_ge(ctx_hi_done, b * (N2 // KG) + c + 1)
                    pool.tensor_tensor(ctx_lo[:, :, at], ctx_raw[:, c % 2, :, :],
                                       ctx_hi[:, :, at].bitcast(F32), ALU.subtract).then_inc(ctx_split, 1)
                with pool.Fori(0, PAIRS) as p:
                    pool.wait_ge(v_projected, (b * PAIRS + p) * NG + NG + OPEN)
                    split_pair(b * PAIRS + p + 1)

        @block.scalar
        def _(act):
            for opened in (v_stored, heads_T_done, exp_done):
                act.sem_inc(opened, OPEN)
            norm.root(act, 0)
            with act.Fori(0, B) as b:
                with act.Fori(0, PAIRS) as p:
                    u = b * PAIRS + p
                    act.wait_ge(pv_done, u * KT + OPEN)
                    for g in range(NG):
                        k0, n = group_keys(g)
                        act.wait_ge(k_projected, u * NG + g + 1)
                        nc.scalar.activation(keys[0][0:HD, k0:k0 + n], k_bank[g % 2][0:HD, 0:n],
                                             ACT.Copy).then_inc(k_hi_done, 1)
                        nc.scalar.activation(keys[1][HD:P, k0:k0 + n], k_bank[g % 2][HD:P, 0:n],
                                             ACT.Copy).then_inc(k_hi_done, 1)
                        act.wait_ge(v_projected, u * NG + g + 1 + OPEN)
                        nc.scalar.activation(
                            vals[:, k0 // P:(k0 + n) // P, :, 0:HD],
                            v_bank[g % 2][:, 0:n].rearrange("p (t h e) -> p t h e", h=2, e=HD),
                            ACT.Copy).then_inc(v_stored, 1)
                    for kt in range(KT):
                        act.wait_ge(scores_ready, u * KT + kt + 1)
                        if kt >= 4:
                            act.wait_ge(pv_done, u * KT + kt - 3 + OPEN)
                        nc.scalar.activation(probs[:, kt % 4, :], s_bank[kt % 4][:, :], ACT.Exp,
                                             scale=HD ** -0.5).then_inc(exp_done, 1)
                for qt in range(QT):
                    act.wait_ge(o_transposed, b * QT + qt + 1)
                    nc.scalar.activation(heads_T[:, qt, :, :],
                                         v_bank[qt][:, :].rearrange("p (c q) -> p c q", c=IC),
                                         ACT.Copy).then_inc(heads_T_done, 1)

        @block.vector
        def _(dve):
            dve.sem_inc(o_normalized, OPEN)
            dve.wait_ge(x_loaded, 48)
            norm.normalize(dve, 0, X1, xl)
            for t in range(TT):
                dve.tensor_tensor(X1[:, t, :], X1[:, t, :], bo_sb[:, :], ALU.add).then_inc(x1_done, 1)
            for t in range(TT):
                dve.wait_ge(xl_transposed, t + 1)
                src = s_bank[t % 4][:, 0:DC * P].rearrange("p (c q) -> p c q", c=DC)
                dve.tensor_copy(xl_T[:, :, t * P:(t + 1) * P], src).then_inc(xl_T_stored, 1)
            with dve.Fori(0, B) as b:
                latents = bass.ds(b * N1, N1)
                dve.tensor_copy(own_hi[:, :, :], xl_T[:, :, latents]).then_inc(own_hi_done, 1)
                dve.wait_ge(own_hi_done, b + 1)
                dve.tensor_tensor(own_lo[:, :, :], xl_T[:, :, latents], own_hi[:, :, :].bitcast(F32),
                                  ALU.subtract).then_inc(own_split, 1)
                with dve.Fori(0, PAIRS) as p:
                    u = b * PAIRS + p
                    dve.wait_ge(pv_done, u * KT + OPEN)
                    dve.wait_ge(q_projected, u + 1)
                    q_ps = v_bank[1][:, :].rearrange("p (h q) -> p h q", h=2)
                    dve.tensor_copy(q_hi[:, :, :], q_ps).then_inc(q_hi_done, 1)
                    dve.wait_ge(q_hi_done, u + 1)
                    dve.tensor_tensor(q_lo[:, :, :], q_ps, q_hi[:, :, :].bitcast(F32),
                                      ALU.subtract).then_inc(q_split, 1)

                    def reduce_max(g):
                        for h in range(2):
                            n = group_keys(g)[1]
                            dve.wait_ge(max_scored, u * (2 * NG) + 2 * g + h + 1)
                            for qt in range(QT):
                                i = dve.tensor_reduce(maxes[:, 2 * h + qt, g:g + 1],
                                                      s_bank[2 * h + qt][:, 0:n], AX_X, ALU.max)
                            i.then_inc(max_reduced, 1)

                    for g in range(NG):
                        k0, n = group_keys(g)
                        for h in range(2):
                            hi, lo = (slice(0, HD), slice(HD, P)) if h == 0 else (slice(HD, P), slice(0, HD))
                            dve.wait_ge(k_hi_done, u * (2 * NG) + 2 * g + h + 1)
                            i = dve.tensor_tensor(keys[h][lo, k0:k0 + n], k_bank[g % 2][hi, 0:n],
                                                  keys[h][hi, k0:k0 + n].bitcast(F32), ALU.subtract)
                        i.then_inc(k_split, 1)
                        if g >= 1:
                            reduce_max(g - 1)
                    reduce_max(NG - 1)
                    dve.wait_ge(max_reduced, u * (2 * NG) + 2 * NG)
                    dve.tensor_reduce(rowmax[:, :], maxes[:, :, :], AX_X, ALU.max).then_inc(rowmax_done, 1)
                    dve.wait_ge(rowmax_done, u + 1)
                    for h in range(2):
                        for qt in range(QT):
                            j = 2 * h + qt
                            dve.tensor_scalar(neg_diag[:, h, qt * P:(qt + 1) * P], ident[:, :],
                                              rowmax[:, j:j + 1], -1.0, ALU.mult,
                                              ALU.mult).then_inc(diag_ready, 1)
                    dve.wait_ge(pv_done, u * KT + KT + OPEN)
                    for h in range(2):
                        sums = k_bank[h][:, 0:QT * (HD + 1)].rearrange("p (t e) -> p t e", t=QT)[:, :, HD]
                        dve.reciprocal(rsum[:, 2 * h:2 * h + 2], sums).then_inc(rsum_done, 1)
                    dve.wait_ge(rsum_done, u * 2 + 2)
                    for h in range(2):
                        for qt in range(QT):
                            j = 2 * h + qt
                            dve.tensor_scalar(heads_out[:, qt, bass.ds(p * P + h * HD, HD)],
                                              k_bank[h][:, qt * (HD + 1):qt * (HD + 1) + HD],
                                              rsum[:, j:j + 1], None, ALU.mult).then_inc(o_normalized, 1)
                for qt in range(QT):
                    dve.wait_ge(out_projected, b * QT + qt + 1)
                    at = bass.ds(b * QT + qt, 1)
                    dve.tensor_tensor(X1[:, at, :], k_bank[qt][:, 0:D].rearrange("p (o d) -> p o d", o=1),
                                      X1[:, at, :], ALU.add).then_inc(x1_done, 1)

        @block.tensor
        def _(pe):
            for opened in (pv_done, v_projected):
                pe.sem_inc(opened, OPEN)
            pe.wait_ge(ident_ready, 1)
            for t in range(TT):
                pe.wait_ge(norm.done, norm.tiles_done(0, t + 1))
                if t >= 4:
                    pe.wait_ge(xl_T_stored, t - 3)
                for c in range(DC):
                    i = pe.transpose(s_bank[t % 4][:, c * P:(c + 1) * P], xl[:, t, c * P:(c + 1) * P], ident[:, :])
                i.then_inc(xl_transposed, 1)
            pe.wait_ge(xl_T_stored, TT)

            def product3(out, lhs, rhs, first=True, last=True):
                n = len(lhs)
                for c in range(n):
                    (lh, ll), (rh, rl) = lhs[c], rhs[c]
                    for k, (l, r) in enumerate(((lh, rh), (lh, rl), (ll, rh))):
                        i = pe.matmul(out, l, r, start=(c == 0 and k == 0), stop=(c == n - 1 and k == 2))
                return i

            with pe.Fori(0, B) as b:
                with pe.Fori(0, PAIRS) as p:
                    u = b * PAIRS + p
                    pe.wait_ge(w_split, u * 3 + 3)
                    pe.wait_ge(v_stored, u * NG + OPEN)
                    pe.wait_ge(heads_T_done, b * QT + OPEN)
                    pe.wait_ge(own_split, b + 1)
                    for h in range(2):
                        i = product3(v_bank[1][:, h * N1:(h + 1) * N1],
                                     [(q_w_hi[:, c, h, :, :].rearrange("p a e -> p (a e)"),
                                       q_w_lo[:, c, h, :, :].rearrange("p a e -> p (a e)")) for c in range(DC)],
                                     [(own_hi[:, c, :], own_lo[:, c, :]) for c in range(DC)])
                    i.then_inc(q_projected, 1)
                    pe.wait_ge(o_normalized, u * 4 + OPEN)
                    pe.wait_ge(x1_done, b * QT + TT)
                    pe.wait_ge(exp_done, u * KT + OPEN)

                    def score_for_max(g):
                        k0, n = group_keys(g)
                        pe.wait_ge(k_split, u * NG + g + 1)
                        if g == 0:
                            pe.wait_ge(q_split, u + 1)
                        for h in range(2):
                            if g >= 1:
                                pe.wait_ge(max_reduced, u * (2 * NG) + 2 * g - 1 + h)
                            for qt in range(QT):
                                i = pe.matmul(s_bank[2 * h + qt][:, 0:n], q_hi[:, h, qt * P:(qt + 1) * P],
                                              keys[h][:, k0:k0 + n], start=True, stop=True)
                            i.then_inc(max_scored, 1)

                    for g in range(NG):
                        k0, n = group_keys(g)
                        kind = 0 if g == 0 else 1
                        if g >= 1:
                            pe.wait_ge(ctx_split, b * (N2 // KG) + g + OPEN)
                        if g >= 2:
                            pe.wait_ge(k_split, u * NG + g - 1)
                        if g == 0:
                            rhs = [(own_hi[:, c, :], own_lo[:, c, :]) for c in range(DC)]
                        else:
                            at = slice((g - 1) * KG, g * KG)
                            rhs = [(ctx_hi[:, c, at], ctx_lo[:, c, at]) for c in range(DC)]
                        product3(k_bank[g % 2][:, 0:n],
                                 [(w_hi[:, kind, c, :], w_lo[:, kind, c, :]) for c in range(DC)],
                                 rhs).then_inc(k_projected, 1)
                        if g == 1:
                            pe.wait_ge(q_split, u + 1)
                        if g >= 2:
                            pe.wait_ge(v_stored, u * NG + g - 1 + OPEN)
                        for t in range(n // P):
                            if g == 0:
                                lhs = [(own_hi[:, c, t * P:(t + 1) * P], own_lo[:, c, t * P:(t + 1) * P])
                                       for c in range(DC)]
                            else:
                                at = slice((g - 1) * KG + t * P, (g - 1) * KG + (t + 1) * P)
                                lhs = [(ctx_hi[:, c, at], ctx_lo[:, c, at]) for c in range(DC)]
                            i = product3(v_bank[g % 2][:, t * P:(t + 1) * P], lhs,
                                         [(w_hi[:, 2 + kind, c, :], w_lo[:, 2 + kind, c, :]) for c in range(DC)])
                        i.then_inc(v_projected, 1)
                        if g >= 1:
                            score_for_max(g - 1)
                    score_for_max(NG - 1)

                    pe.wait_ge(diag_ready, u * 4 + 4)
                    pe.wait_ge(v_stored, u * NG + NG + OPEN)
                    for kt in range(KT + LAG):
                        if kt < KT:
                            if kt >= 4:
                                pe.wait_ge(exp_done, u * KT + kt - 3 + OPEN)
                            at = slice(kt * P, (kt + 1) * P)
                            for h in range(2):
                                out = s_bank[kt % 4][:, h * N1:(h + 1) * N1]
                                pe.matmul(out, keys[h][:, at], q_hi[:, h, :], start=True, stop=False)
                                pe.matmul(out, keys[h][:, at], q_lo[:, h, :], start=False, stop=False)
                                i = pe.matmul(out, ones[:, :], neg_diag[:, h, :], start=False, stop=True)
                            i.then_inc(scores_ready, 1)
                        if kt >= LAG:
                            t = kt - LAG
                            pe.wait_ge(exp_done, u * KT + t + 1 + OPEN)
                            for h in range(2):
                                for qt in range(QT):
                                    at = slice(h * N1 + qt * P, h * N1 + (qt + 1) * P)
                                    i = pe.matmul(k_bank[h][:, qt * (HD + 1):(qt + 1) * (HD + 1)],
                                                  probs[:, t % 4, at], vals[:, t, h, :],
                                                  start=(t == 0 and qt == 0), stop=(t == KT - 1),
                                                  skip_group_check=True)
                            i.then_inc(pv_done, 1)
                pe.wait_ge(o_normalized, (b + 1) * (4 * PAIRS) + OPEN)
                for qt in range(QT):
                    for c in range(IC):
                        i = pe.transpose(v_bank[qt][:, c * P:(c + 1) * P],
                                         heads_out[:, qt, c * P:(c + 1) * P], ident[:, :])
                    i.then_inc(o_transposed, 1)
                for qt in range(QT):
                    pe.wait_ge(heads_T_done, b * QT + qt + 1 + OPEN)
                    for c in range(IC):
                        i = pe.matmul(k_bank[qt][:, 0:D], heads_T[:, qt, c, :], wo_sb[:, c, :],
                                      start=(c == 0), stop=(c == IC - 1))
                    i.then_inc(out_projected, 1)


def route_and_project(nc, w, X1, perm_T, xi, z_gate, mixed, ident, banks):
    ctx = ExitStack()
    with ctx:
        def sb(name, shape, dt=F32):
            return ctx.enter_context(nc.sbuf_tensor(f"mx_{name}", shape, dt))

        def sem(name):
            return ctx.enter_context(nc.semaphore(f"mx_{name}"))

        lnw = sb("lnw", [P, D])
        lnb = sb("lnb", [P, D])
        rw1 = sb("rw1", [P, DC, RH])
        rb1 = sb("rb1", [P, 1])
        rw2 = sb("rw2", [P, 1])
        rb2 = sb("rb2", [P, 1])
        wq = sb("wq", [P, DC, D])
        wk = sb("wk", [P, DC, D])
        wv = sb("wv", [P, DC, D])
        wo = sb("wo", [P, DC, D])
        bq = sb("bq", [P, DC])
        bk = sb("bk", [P, DC])
        bv = sb("bv", [P, D])
        bo = sb("bo", [P, D])
        in_w = sb("in_w", [P, DC, 2 * DIN])
        y = sb("y", [P, TT, D])
        xn = sb("xn", [P, TT, D])
        xn_T = sb("xn_T", [P, DC, B * N1])
        z = sb("z", [P, B * N1])
        z2 = sb("z2", [P, B * N1])
        th = sb("th", [P, B * N1])
        rw2_bc = sb("rw2_bc", [P, P])
        score = sb("score", [P, B * N1])
        own = sb("own", [P, TT, P])
        score_col = sb("score_col", [P, TT])
        above = sb("above", [P, TT, N1])
        ties = sb("ties", [P, TT, N1])
        rank = sb("rank", [P, TT])
        other = sb("other", [P, TT])
        base = sb("base", [P, TT])
        diff = sb("diff", [P, TT])
        diff2 = sb("diff2", [P, TT])
        place = sb("place", [P, TT])
        ones = sb("ones", [P, P])
        before = sb("before", [P, P])
        earlier = sb("earlier", [P, QT, N1])
        columns = sb("columns", [P, N1])
        perm = sb("perm", [P, TT, N1])
        xp = sb("xp", [P, DC, B, N1])
        xa = sb("xa", [P, DC, B, 2, TOP])
        q_T = sb("q_T", [P, DC, B, 2 * TOP])
        k_T = sb("k_T", [P, DC, B, TOP])
        head_mask = sb("head_mask", [P, HC])
        pair_mask = sb("pair_mask", [P, D // 2 // AHD, 2, AHD])
        k_heads = sb("k_heads", [P, DC, HC, TOP])
        k_heads2 = sb("k_heads2", [P, DC, HC, TOP])
        v_biased = sb("v_biased", [P, 2, D])
        v2 = sb("v2", [P, B, D])
        top = sb("top", [P, B, AH])
        e = sb("e", [P, 2, AH, TOP])
        esum = sb("esum", [P, B, AH])
        rsum = sb("rsum", [P, B, AH])
        probs = sb("probs", [P, 2, AH, TOP])
        probs_T = sb("probs_T", [P, 2, AH // 2, P])
        o = sb("o", [P, 2, D])
        o_T = sb("o_T", [P, 2, DC, P])
        zt = sb("zt", [P, 2, 2 * NS])
        norm = Norm(sb, sem, "norm", TT)

        loaded = sem("loaded")
        consts = sem("consts")
        masked = sem("masked")
        columns_ready = sem("columns_ready")
        rw2_ready = sem("rw2_ready")
        x1_added = sem("x1_added")
        weighted = sem("weighted")
        xn_ready = sem("xn_ready")
        xn_transposed = sem("xn_transposed")
        xn_T_stored = sem("xn_T_stored")
        hidden = sem("hidden")
        z_stored = sem("z_stored")
        gelu_in = sem("gelu_in")
        tanh_done = sem("tanh_done")
        gelu_done = sem("gelu_done")
        scored = sem("scored")
        score_stored = sem("score_stored")
        own_done = sem("own_done")
        score_col_done = sem("score_col_done")
        ties_done = sem("ties_done")
        above_done = sem("above_done")
        rank_done = sem("rank_done")
        other_done = sem("other_done")
        counted = sem("counted")
        place_step = sem("place_step")
        perm_done = sem("perm_done")
        perm_transposed = sem("perm_transposed")
        perm_T_stored = sem("perm_T_stored")
        permuted = sem("permuted")
        xp_stored = sem("xp_stored")
        xa_stored = sem("xa_stored")
        qk_projected = sem("qk_projected")
        qk_stored = sem("qk_stored")
        v_projected = sem("v_projected")
        v_biased_done = sem("v_biased_done")
        v2_done = sem("v2_done")
        inner_projected = sem("inner_projected")
        xi_stored = sem("xi_stored")
        z_tanh = sem("z_tanh")
        z_done = sem("z_done")
        k_heads_done = sem("k_heads_done")
        a_scored = sem("a_scored")
        top_done = sem("top_done")
        shifted = sem("shifted")
        exp_done = sem("exp_done")
        esum_done = sem("esum_done")
        rsum_done = sem("rsum_done")
        probs_done = sem("probs_done")
        probs_transposed = sem("probs_transposed")
        probs_T_stored = sem("probs_T_stored")
        o_ready = sem("o_ready")
        o_stored = sem("o_stored")
        o_transposed = sem("o_transposed")
        o_T_stored = sem("o_T_stored")
        a_out = sem("a_out")
        mixed_done = sem("mixed_done")

        block = ctx.enter_context(nc.Block())

        @block.sync
        def _(sp):
            def row(v):
                return v.rearrange("(a d) -> a d", a=1).broadcast_to([P, v.shape[0]])

            chunks = "(c p) n -> p c n"
            for dst, src in ((lnw[:, :], row(w["ln_w"])), (lnb[:, :], row(w["ln_b"])),
                             (rw1[:, :, :], w["r_w1"].rearrange(chunks, p=P)),
                             (rb1[:, :], w["r_b1"].rearrange("(p a) -> p a", a=1)), (rw2[:, :], w["r_w2"]),
                             (rb2[:, :], row(w["r_b2"])),
                             (wq[:, :, :], w["Wq"].rearrange(chunks, p=P)),
                             (wk[:, :, :], w["Wk"].rearrange(chunks, p=P)),
                             (wv[:, :, :], w["Wv"].rearrange(chunks, p=P)),
                             (wo[:, :, :], w["Wo"].rearrange(chunks, p=P)),
                             (bq[:, :], w["bq"]),
                             (bk[:, :], w["bk"]),
                             (bv[:, :], row(w["bv"])), (bo[:, :], row(w["bo"])),
                             (in_w[:, :, :], w["in_w"].rearrange(chunks, p=P))):
                sp.dma_start(dst, src).then_inc(loaded, 16)

        LOADS = 15

        @block.gpsimd
        def _(pool):
            pool.memset(ones[:, :], 1.0).then_inc(consts, 1)
            pool.memset(before[:, :], 1.0).then_inc(consts, 1)
            pool.memset(earlier[:, :, :], 1.0).then_inc(consts, 1)
            pool.memset(head_mask[:, :], 1.0).then_inc(consts, 1)
            pool.memset(pair_mask[:, :, :, :], 1.0).then_inc(consts, 1)
            pool.memset(xi[:, :, :, 0:DCONV - 1], 0.0).then_inc(consts, 1)
            pool.iota(columns[:, :], pattern=[[1, N1]], base=0, channel_multiplier=0,
                      allow_small_or_imprecise_dtypes=True).then_inc(columns_ready, 1)
            pool.wait_ge(consts, 6)
            pool.affine_select(out=before[:, :], in_=before[:, :], compare_op=ALU.is_gt, fill=0.0,
                               base=0, pattern=[[1, P]], channel_multiplier=-1).then_inc(masked, 1)
            pool.affine_select(out=earlier[:, :, :], in_=earlier[:, :, :], compare_op=ALU.is_gt, fill=0.0,
                               base=0, pattern=[[P, QT], [-1, N1]], channel_multiplier=1).then_inc(masked, 1)
            pool.affine_select(out=head_mask[:, :], in_=head_mask[:, :], compare_op=ALU.is_ge, fill=0.0,
                               base=0, pattern=[[-AHD, HC]], channel_multiplier=1).then_inc(masked, 1)
            for h, (op, at) in enumerate(((ALU.is_ge, TOP - 1), (ALU.is_ge, -TOP))):
                part = pair_mask[:, :, h, :]
                pool.affine_select(out=part, in_=part, compare_op=op, fill=0.0, base=at,
                                   pattern=[[0, D // 2 // AHD], [0, AHD]],
                                   channel_multiplier=-1 if h == 0 else 1).then_inc(masked, 1)
            pool.wait_ge(masked, 3)
            pool.affine_select(out=head_mask[:, :], in_=head_mask[:, :], compare_op=ALU.is_ge, fill=0.0,
                               base=AHD - 1, pattern=[[AHD, HC]], channel_multiplier=-1).then_inc(masked, 1)
            pool.wait_ge(norm.done, norm.tiles_done(0, TT))
            pool.tensor_tensor(X1[:, :, :], X1[:, :, :], y[:, :, :], ALU.add).then_inc(x1_added, 1)
            for b in range(B):
                pool.wait_ge(xp_stored, b + 1)
                for dup in range(2):
                    pool.tensor_copy(xa[:, :, b, dup, :], xp[:, :, b, NS:N1]).then_inc(xa_stored, 1)
            pool.wait_ge(masked, 6)
            for b in range(B):
                kh = (k_heads, k_heads2)[b % 2]
                pool.wait_ge(qk_stored, 2 * DC)
                if b >= 2:
                    pool.wait_ge(a_scored, b - 1)
                for c in range(DC):
                    pool.tensor_tensor(kh[:, c, :, :],
                                       k_T[:, c, b, :].unsqueeze(1).broadcast_to([P, HC, TOP]),
                                       head_mask[:, :].unsqueeze(2).broadcast_to([P, HC, TOP]),
                                       ALU.mult).then_inc(k_heads_done, 1)

        @block.scalar
        def _(act):
            norm.root(act, 0)
            norm.root(act, 1)
            for t in range(TT):
                act.wait_ge(xn_transposed, t + 1)
                nc.scalar.activation(xn_T[:, :, t * P:(t + 1) * P],
                                     banks[t][:, 0:DC * P].rearrange("p (c q) -> p c q", c=DC),
                                     ACT.Copy).then_inc(xn_T_stored, 1)
            act.wait_ge(loaded, 16 * LOADS)
            for n in range(2):
                act.wait_ge(hidden, n + 1)
                nc.scalar.activation(z[:, n * 512:(n + 1) * 512], banks[n][:, :], ACT.Identity,
                                     bias=rb1[:, 0:1]).then_inc(z_stored, 1)
            act.wait_ge(gelu_in, 1)
            nc.scalar.activation(th[:, :], z2[:, :], ACT.Tanh, scale=GELU).then_inc(tanh_done, 1)
            for b in range(B):
                act.wait_ge(perm_transposed, b + 1)
                nc.scalar.activation(perm_T[:, b, :, :], banks[4 + b][:, :].rearrange(
                    "p (a t) -> p a t", a=2), ACT.Copy).then_inc(perm_T_stored, 1)
            for c in range(DC):
                act.wait_ge(qk_projected, 2 * c + 1)
                nc.scalar.activation(q_T[:, c, :, :], banks[2 * c][:, :].rearrange("p (b q) -> p b q", b=B),
                                     ACT.Identity, bias=bq[:, c:c + 1]).then_inc(qk_stored, 1)
                act.wait_ge(qk_projected, 2 * c + 2)
                nc.scalar.activation(k_T[:, c, :, :], banks[2 * c + 1][:, 0:B * TOP].rearrange(
                    "p (b q) -> p b q", b=B), ACT.Identity, bias=bk[:, c:c + 1]).then_inc(qk_stored, 1)
            for n in range(2 * CT * 2):
                ct, half = n // 2, n % 2
                act.wait_ge(inner_projected, n + 1)
                bank = banks[n % 4][:, 0:2 * NS]
                if ct < CT:
                    nc.scalar.activation(xi[:, ct, 2 * half:2 * half + 2, DCONV - 1:],
                                         bank.rearrange("p (b t) -> p b t", b=2), ACT.Copy).then_inc(xi_stored, 1)
                else:
                    m = n - 2 * CT
                    if m >= 2:
                        act.wait_ge(z_done, m - 1)
                    nc.scalar.activation(zt[:, m % 2, :], bank, ACT.Tanh, scale=0.5).then_inc(z_tanh, 1)
            for b in range(B):
                act.wait_ge(shifted, b + 1)
                nc.scalar.activation(e[:, b % 2, :, :], e[:, b % 2, :, :], ACT.Exp,
                                     scale=AHD ** -0.5).then_inc(exp_done, 1)
                if b >= 2:
                    act.wait_ge(o_ready, b - 1)
                for n in range(2):
                    act.wait_ge(probs_transposed, 2 * b + n + 1)
                    nc.scalar.activation(probs_T[:, b % 2, 4 * n:4 * n + 4, :],
                                         banks[4 + n][:, :].rearrange("p (a q) -> p a q", a=4),
                                         ACT.Copy).then_inc(probs_T_stored, 1)
                act.wait_ge(o_ready, b + 1)
                nc.scalar.activation(o[:, b % 2, :], banks[6][:, 0:D], ACT.Copy).then_inc(o_stored, 1)
                act.wait_ge(o_transposed, b + 1)
                nc.scalar.activation(o_T[:, b % 2, :, :], banks[7][:, 0:DC * P].rearrange(
                    "p (c q) -> p c q", c=DC), ACT.Copy).then_inc(o_T_stored, 1)

        @block.vector
        def _(dve):
            norm.normalize(dve, 0, X1, y)
            dve.wait_ge(norm.done, norm.tiles_done(0, TT))
            norm.normalize(dve, 1, y, xn)
            dve.wait_ge(norm.done, norm.tiles_done(1, TT))
            dve.wait_ge(loaded, 16 * LOADS)
            dve.tensor_tensor(xn[:, :, :], xn[:, :, :], lnw[:, :].unsqueeze(1).broadcast_to([P, TT, D]),
                              ALU.mult).then_inc(weighted, 1)
            dve.wait_ge(weighted, 1)
            for t in range(TT):
                dve.tensor_tensor(xn[:, t, :], xn[:, t, :], lnb[:, :], ALU.add).then_inc(xn_ready, 1)
            dve.wait_ge(consts, 6)
            dve.tensor_scalar(rw2_bc[:, :], ones[:, :], rw2[:, 0:1], None, ALU.mult).then_inc(rw2_ready, 1)
            dve.wait_ge(z_stored, 2)
            dve.tensor_tensor(z2[:, :], z[:, :], z[:, :], ALU.mult).then_inc(place_step, 1)
            dve.wait_ge(place_step, 1)
            dve.tensor_scalar(z2[:, :], z2[:, :], 0.044715, 1.0, ALU.mult, ALU.add).then_inc(place_step, 1)
            dve.wait_ge(place_step, 2)
            dve.tensor_tensor(z2[:, :], z2[:, :], z[:, :], ALU.mult).then_inc(gelu_in, 1)
            dve.wait_ge(tanh_done, 1)
            dve.scalar_tensor_tensor(z[:, :], th[:, :], 1.0, z[:, :], ALU.add, ALU.mult).then_inc(gelu_done, 1)
            for n in range(2):
                dve.wait_ge(scored, n + 1)
                dve.tensor_scalar(score[:, n * 512:(n + 1) * 512], banks[2 + n][:, :], 0.5, rb2[:, 0:1],
                                  ALU.mult, ALU.add).then_inc(score_stored, 1)
            dve.wait_ge(score_stored, 2)
            dve.tensor_tensor(own[:, :, :], score[:, :].rearrange("p (t j) -> p t j", t=TT),
                              ident[:, :].unsqueeze(1).broadcast_to([P, TT, P]), ALU.mult).then_inc(own_done, 1)
            dve.wait_ge(own_done, 1)
            dve.tensor_reduce(score_col[:, :], own[:, :, :], AX_X, ALU.add).then_inc(score_col_done, 1)
            dve.wait_ge(score_col_done, 1)
            dve.wait_ge(masked, 6)
            for t in range(TT):
                all_scores = score[:, (t // QT) * N1:(t // QT + 1) * N1]
                dve.scalar_tensor_tensor(ties[:, t, :], all_scores, score_col[:, t:t + 1],
                                         earlier[:, t % QT, :], ALU.is_equal, ALU.mult).then_inc(ties_done, 1)
            for t in range(TT):
                all_scores = score[:, (t // QT) * N1:(t // QT + 1) * N1]
                dve.wait_ge(ties_done, t + 1)
                dve.scalar_tensor_tensor(above[:, t, :], all_scores, score_col[:, t:t + 1],
                                         ties[:, t, :], ALU.is_gt, ALU.add).then_inc(above_done, 1)
            dve.wait_ge(above_done, TT)
            dve.tensor_reduce(rank[:, :], above[:, :, :], AX_X, ALU.add).then_inc(rank_done, 1)
            dve.wait_ge(rank_done, 1)
            dve.tensor_scalar(other[:, :], rank[:, :], float(TOP), None, ALU.is_ge).then_inc(other_done, 1)
            dve.tensor_scalar(base[:, :], rank[:, :], float(NS), None, ALU.add).then_inc(place_step, 1)
            dve.wait_ge(counted, 1)
            dve.wait_ge(place_step, 3)
            dve.tensor_tensor(diff[:, :].rearrange("p (b t) -> p t b", t=QT),
                              banks[0][:, 0:TT].rearrange("p (t b) -> p t b", t=QT),
                              base[:, :].rearrange("p (b t) -> p t b", t=QT), ALU.subtract).then_inc(place_step, 1)
            dve.wait_ge(place_step, 4)
            dve.wait_ge(other_done, 1)
            dve.tensor_tensor(diff2[:, :], diff[:, :], other[:, :], ALU.mult).then_inc(place_step, 1)
            dve.wait_ge(place_step, 5)
            dve.tensor_tensor(place[:, :], diff2[:, :], base[:, :], ALU.add).then_inc(place_step, 1)
            dve.wait_ge(place_step, 6)
            dve.wait_ge(columns_ready, 1)
            for t in range(TT):
                dve.tensor_scalar(perm[:, t, :], columns[:, :], place[:, t:t + 1], None,
                                  ALU.is_equal).then_inc(perm_done, 1)
            for b in range(B):
                dve.wait_ge(permuted, b + 1)
                dve.tensor_copy(xp[:, :, b, :], banks[b][:, :].rearrange("p (c q) -> p c q", c=DC)
                                ).then_inc(xp_stored, 1)
            for b in range(B):
                dve.wait_ge(v_projected, b + 1)
                if b >= 2:
                    dve.wait_ge(v2_done, b - 1)
                dve.tensor_tensor(v_biased[:, b % 2, :], banks[4 + b % 2][:, 0:D], bv[:, :],
                                  ALU.add).then_inc(v_biased_done, 1)
                dve.wait_ge(v_biased_done, b + 1)
                dve.tensor_tensor(v2[:, b, :], v_biased[:, b % 2, :],
                                  pair_mask[:, :, :, :].rearrange("p a h e -> p (a h e)"),
                                  ALU.mult).then_inc(v2_done, 1)
            for m in range(2 * CT):
                n = 2 * CT + m
                dve.wait_ge(z_tanh, m + 1)
                dve.scalar_tensor_tensor(
                    z_gate[:, m // 2, 2 * (m % 2):2 * (m % 2) + 2, :],
                    zt[:, m % 2, :].rearrange("p (b t) -> p b t", b=2), 1.0,
                    banks[n % 4][:, 0:2 * NS].rearrange("p (b t) -> p b t", b=2),
                    ALU.add, ALU.mult).then_inc(z_done, 1)
            for b in range(B):
                s = [banks[2 * (b % 2) + c][:, :].rearrange("p (h k) -> p h k", h=HC) for c in range(DC)]
                dve.wait_ge(a_scored, b + 1)
                for c in range(DC):
                    dve.tensor_reduce(top[:, b, c * HC:(c + 1) * HC], s[c], AX_X, ALU.max).then_inc(top_done, 1)
                if b >= 2:
                    dve.wait_ge(probs_done, b - 1)
                dve.wait_ge(top_done, 2 * b + 2)
                for c in range(DC):
                    i = dve.tensor_tensor(e[:, b % 2, c * HC:(c + 1) * HC, :], s[c],
                                          top[:, b, c * HC:(c + 1) * HC].unsqueeze(2).broadcast_to([P, HC, TOP]),
                                          ALU.subtract)
                i.then_inc(shifted, 1)
                dve.wait_ge(exp_done, b + 1)
                dve.tensor_reduce(esum[:, b, :], e[:, b % 2, :, :], AX_X, ALU.add).then_inc(esum_done, 1)
                dve.wait_ge(esum_done, b + 1)
                dve.reciprocal(rsum[:, b, :], esum[:, b, :]).then_inc(rsum_done, 1)
                dve.wait_ge(rsum_done, b + 1)
                if b >= 2:
                    dve.wait_ge(probs_transposed, 2 * b - 2)
                dve.tensor_tensor(probs[:, b % 2, :, :], e[:, b % 2, :, :],
                                  rsum[:, b, :].unsqueeze(2).broadcast_to([P, AH, TOP]),
                                  ALU.mult).then_inc(probs_done, 1)
                if b >= 1:
                    dve.wait_ge(a_out, b)
                    dve.tensor_tensor(mixed[TOP:P, b - 1, 1, :], banks[7][TOP:P, 0:D], bo[TOP:P, :],
                                      ALU.add).then_inc(mixed_done, 1)
            dve.wait_ge(a_out, B)
            dve.tensor_tensor(mixed[TOP:P, B - 1, 1, :], banks[7][TOP:P, 0:D], bo[TOP:P, :],
                              ALU.add).then_inc(mixed_done, 1)

        @block.tensor
        def _(pe):
            for t in range(TT):
                pe.wait_ge(xn_ready, t + 1)
                for c in range(DC):
                    i = pe.transpose(banks[t][:, c * P:(c + 1) * P], xn[:, t, c * P:(c + 1) * P], ident[:, :])
                i.then_inc(xn_transposed, 1)
            pe.wait_ge(loaded, 16 * LOADS)
            pe.wait_ge(xn_T_stored, TT)
            for n in range(2):
                for c in range(DC):
                    i = pe.matmul(banks[n][:, :], rw1[:, c, :], xn_T[:, c, n * 512:(n + 1) * 512],
                                  start=(c == 0), stop=(c == DC - 1))
                i.then_inc(hidden, 1)
            pe.wait_ge(rw2_ready, 1)
            pe.wait_ge(gelu_done, 1)
            for n in range(2):
                pe.matmul(banks[2 + n][:, :], rw2_bc[:, :], z[:, n * 512:(n + 1) * 512],
                          start=True, stop=True).then_inc(scored, 1)
            pe.wait_ge(other_done, 1)
            pe.wait_ge(consts, 6)
            pe.wait_ge(masked, 6)
            pe.wait_ge(z_stored, 2)
            o3 = other[:, :].rearrange("p (b t) -> p b t", t=QT)
            pe.matmul(banks[0][:, 0:B], before[:, :], o3[:, :, 0], start=True, stop=True)
            pe.matmul(banks[0][:, B:2 * B], ones[:, :], o3[:, :, 0], start=True, stop=False)
            pe.matmul(banks[0][:, B:2 * B], before[:, :], o3[:, :, 1], start=False, stop=True).then_inc(counted, 1)
            pe.wait_ge(place_step, 4)
            for b in range(B):
                pe.wait_ge(perm_done, QT * (b + 1))
                for c in range(DC):
                    for t in range(QT):
                        i = pe.matmul(banks[b][:, c * N1:(c + 1) * N1], xn[:, QT * b + t, c * P:(c + 1) * P],
                                      perm[:, QT * b + t, :], start=(t == 0), stop=(t == QT - 1))
                i.then_inc(permuted, 1)
                for a in range(2):
                    for t in range(QT):
                        i = pe.transpose(banks[4 + b][:, a * N1 + t * P:a * N1 + (t + 1) * P],
                                         perm[:, QT * b + t, a * P:(a + 1) * P], ident[:, :])
                i.then_inc(perm_transposed, 1)
            pe.wait_ge(xa_stored, 2 * B)
            for c in range(DC):
                for d in range(DC):
                    i = pe.matmul(banks[2 * c][:, :], wq[:, d, c * P:(c + 1) * P],
                                  xa[:, d, :, :, :].rearrange("p b a q -> p (b a q)"),
                                  start=(d == 0), stop=(d == DC - 1))
                i.then_inc(qk_projected, 1)
                for d in range(DC):
                    i = pe.matmul(banks[2 * c + 1][:, 0:B * TOP], wk[:, d, c * P:(c + 1) * P],
                                  xa[:, d, :, 0, :], start=(d == 0), stop=(d == DC - 1))
                i.then_inc(qk_projected, 1)
            pe.wait_ge(perm_T_stored, B)
            for b in range(B):
                if b >= 2:
                    pe.wait_ge(v_biased_done, b - 1)
                for d in range(DC):
                    i = pe.matmul(banks[4 + b % 2][:, 0:D], xa[:, d, b, :, :].rearrange("p a q -> p (a q)"),
                                  wv[:, d, :], start=(d == 0), stop=(d == DC - 1))
                i.then_inc(v_projected, 1)
            pe.wait_ge(qk_stored, 2 * DC)
            for n in range(2 * CT * 2):
                ct, half = n // 2, n % 2
                if 4 <= n < 2 * CT + 4:
                    pe.wait_ge(xi_stored, n - 3)
                elif n >= 2 * CT + 4:
                    pe.wait_ge(z_done, n - 3 - 2 * CT)
                for d in range(DC):
                    i = pe.matmul(banks[n % 4][:, 0:2 * NS], in_w[:, d, ct * P:(ct + 1) * P],
                                  xp[:, d, 2 * half:2 * half + 2, 0:NS], start=(d == 0), stop=(d == DC - 1))
                i.then_inc(inner_projected, 1)
            pe.wait_ge(z_done, 2 * CT)
            pe.wait_ge(v2_done, B)

            def attend_scores(b):
                pe.wait_ge(k_heads_done, DC * (b + 1))
                if b >= 2:
                    pe.wait_ge(shifted, b - 1)
                for c in range(DC):
                    i = pe.matmul(banks[2 * (b % 2) + c][:, :], q_T[:, c, b, :],
                                  (k_heads, k_heads2)[b % 2][:, c, :, :].rearrange("p h k -> p (h k)"),
                                  start=True, stop=True)
                i.then_inc(a_scored, 1)

            attend_scores(0)
            for b in range(B):
                if b + 1 < B:
                    attend_scores(b + 1)
                pe.wait_ge(probs_done, b + 1)
                flat = probs[:, b % 2, :, :].rearrange("p h k -> p (h k)")
                for n in range(2):
                    if b >= 1:
                        pe.wait_ge(probs_T_stored, 2 * b - 1 + n)
                    for a in range(4):
                        pair = 4 * n + a
                        i = pe.transpose(banks[4 + n][:, a * P:(a + 1) * P],
                                         flat[:, pair * P:(pair + 1) * P], ident[:, :])
                    i.then_inc(probs_transposed, 1)
                pe.wait_ge(probs_T_stored, 2 * b + 2)
                if b >= 1:
                    pe.wait_ge(o_stored, b)
                for pair in range(AH // 2):
                    i = pe.matmul(banks[6][:, pair * 2 * AHD:(pair + 1) * 2 * AHD], probs_T[:, b % 2, pair, :],
                                  v2[:, b, pair * 2 * AHD:(pair + 1) * 2 * AHD], start=True, stop=True)
                i.then_inc(o_ready, 1)
                pe.wait_ge(o_stored, b + 1)
                if b >= 1:
                    pe.wait_ge(mixed_done, b)
                for c in range(DC):
                    i = pe.transpose(banks[7][:, c * P:(c + 1) * P], o[:, b % 2, c * P:(c + 1) * P], ident[:, :])
                i.then_inc(o_transposed, 1)
                pe.wait_ge(o_T_stored, b + 1)
                for c in range(DC):
                    i = pe.matmul(banks[7][:, 0:D], o_T[:, b % 2, c, :], wo[:, c, :],
                                  start=(c == 0), stop=(c == DC - 1))
                i.then_inc(a_out, 1)


def state_space(nc, w, X1, perm_T, xi, z_gate, mixed, ident, banks):
    ctx = ExitStack()
    with ctx:
        def sb(name, shape, dt=F32):
            return ctx.enter_context(nc.sbuf_tensor(f"ss_{name}", shape, dt))

        def sem(name):
            return ctx.enter_context(nc.semaphore(f"ss_{name}"))

        NT = B * NS
        HT = NT // 2
        conv_w = sb("conv_w", [P, CT, DCONV])
        conv_b = sb("conv_b", [P, CT])
        xproj_w = sb("xproj_w", [P, CT, RANK])
        dt_w = sb("dt_w", [DTR, DIN])
        dt_b = sb("dt_b", [P, CT])
        a_log = sb("a_log", [P, CT, DS])
        a_neg = sb("a_neg", [P, CT, DS])
        skip = sb("skip", [P, CT])
        out_w = sb("out_w", [P, CT, D])
        xc = sb("xc", [P, CT, NT])
        delta = sb("delta", [P, CT, NT])
        proj = sb("proj", [RANK, NT])
        bc = sb("bc", [P, 2 * DS, NT])
        decay = [sb(f"decay{i}", [P, B, NS]) for i in range(2)]
        drive = [sb(f"drive{i}", [P, NT]) for i in range(2)]
        state = [sb(f"state{i}", [P, NT]) for i in range(2)]
        dx = xi[:, :, :, :].rearrange("p c b t -> p (c b t)")[:, 0:CT * NT].rearrange("p (c n) -> p c n", c=CT)

        loaded = sem("loaded")
        conv_done = sem("conv_done")
        conv_tanh = sem("conv_tanh")
        half_done = sem("half_done")
        xc_done = sem("xc_done")
        projected = sem("projected")
        proj_stored = sem("proj_stored")
        dt_projected = sem("dt_projected")
        dt_biased = sem("dt_biased")
        soft = sem("soft")
        delta_done = sem("delta_done")
        dx_done = sem("dx_done")
        a_exp = sem("a_exp")
        a_ready = sem("a_ready")
        spread = sem("spread")
        bc_stored_a = sem("bc_stored_a")
        bc_stored_v = sem("bc_stored_v")
        zeroed = sem("zeroed")
        decay_done = sem("decay_done")
        drive_done = sem("drive_done")
        scanned = sem("scanned")
        read_out = sem("read_out")
        summed = sem("summed")
        skipped = sem("skipped")
        gated = sem("gated")
        out_projected = sem("out_projected")
        mixed_done = sem("mixed_done")
        scattered = sem("scattered")
        added = sem("added")

        LOADS = 8
        block = ctx.enter_context(nc.Block())

        @block.sync
        def _(sp):
            for dst, src in ((conv_w[:, :, :], w["conv_w"].rearrange("(c p) k -> p c k", p=P)),
                             (conv_b[:, :], w["conv_b"]),
                             (xproj_w[:, :, :], w["xproj_w"].rearrange("(c p) k -> p c k", p=P)),
                             (dt_w[:, :], w["dt_w"]),
                             (dt_b[:, :], w["dt_b"]),
                             (a_log[:, :, :], w["A_log"].rearrange("(c p) k -> p c k", p=P)),
                             (skip[:, :], w["Dp"]),
                             (out_w[:, :, :], w["out_w"].rearrange("(c p) k -> p c k", p=P))):
                sp.dma_start(dst, src).then_inc(loaded, 16)

        @block.gpsimd
        def _(pool):
            for i in range(2):
                pool.memset(decay[i][:, :, 0:1], 0.0).then_inc(zeroed, 1)
            for ct in range(CT):
                pool.wait_ge(delta_done, ct + 1)
                pool.tensor_tensor(dx[:, ct, :], delta[:, ct, :], xc[:, ct, :], ALU.mult).then_inc(dx_done, 1)
            pool.wait_ge(dx_done, CT)
            for n in range(CT * DS):
                ct, s = n // DS, n % DS
                if ct == 0:
                    pool.wait_ge((bc_stored_a, bc_stored_v)[s % 2], s // 2 + 1)
                if n >= 2:
                    pool.wait_ge(summed, n - 1)
                pool.tensor_tensor(drive[n % 2][:, :], dx[:, ct, :], bc[:, s, :], ALU.mult).then_inc(drive_done, 1)

        @block.scalar
        def _(act):
            for ct in range(CT):
                act.wait_ge(conv_done, ct + 1)
                nc.scalar.activation(delta[:, ct, :], xc[:, ct, :], ACT.Tanh, scale=0.5).then_inc(conv_tanh, 1)
            act.wait_ge(loaded, 16 * LOADS)
            nc.scalar.activation(a_neg[:, :, :], a_log[:, :, :], ACT.Exp).then_inc(a_exp, 1)
            act.wait_ge(projected, 1)
            for h in range(2):
                nc.scalar.activation(proj[:, h * HT:(h + 1) * HT], banks[h][0:RANK, 0:HT],
                                     ACT.Copy).then_inc(proj_stored, 1)
            for ct in range(CT):
                for h in range(2):
                    at = slice(h * HT, (h + 1) * HT)
                    act.wait_ge(dt_projected, 2 * ct + h + 1)
                    nc.scalar.activation(delta[:, ct, at], banks[2 + (2 * ct + h) % 4][:, 0:HT], ACT.Identity,
                                         bias=dt_b[:, ct:ct + 1]).then_inc(dt_biased, 1)
                act.wait_ge(dt_biased, 2 * ct + 2)
                if ct >= 2:
                    act.wait_ge(delta_done, ct - 1)
                part = drive[ct % 2][:, :]
                nc.scalar.activation(part, delta[:, ct, :], ACT.Abs).then_inc(soft, 1)
                act.wait_ge(soft, 3 * ct + 1)
                nc.scalar.activation(part, part, ACT.Exp, scale=-1.0).then_inc(soft, 1)
                act.wait_ge(soft, 3 * ct + 2)
                nc.scalar.activation(part, part, ACT.Ln, bias=1.0).then_inc(soft, 1)
            for r in range(0, 2 * DS, 2):
                for h in range(2):
                    act.wait_ge(spread, 2 * r + h + 1)
                    i = nc.scalar.activation(bc[:, r, h * HT:(h + 1) * HT], banks[2 * (r % 4) + h][:, 0:HT],
                                             ACT.Copy)
                i.then_inc(bc_stored_a, 1)
            act.wait_ge(a_ready, 1)
            act.wait_ge(delta_done, CT)
            act.wait_ge(zeroed, 2)
            for n in range(CT * DS):
                ct, s = n // DS, n % DS
                if n >= 2:
                    act.wait_ge(scanned, n - 1)
                nc.scalar.activation(decay[n % 2][:, :, 1:NS],
                                     delta[:, ct, :].rearrange("p (b t) -> p b t", b=B)[:, :, 1:NS], ACT.Exp,
                                     scale=a_neg[:, ct, s:s + 1]).then_inc(decay_done, 1)

        @block.vector
        def _(dve):
            dve.wait_ge(loaded, 16 * LOADS)
            step = 0
            for ct in range(CT):
                out = xc[:, ct, :].rearrange("p (b t) -> p b t", b=B)
                dve.tensor_scalar(out, xi[:, ct, :, 0:NS], conv_w[:, ct, 0:1], conv_b[:, ct:ct + 1],
                                  ALU.mult, ALU.add).then_inc(half_done, 1)
                for j in range(1, DCONV):
                    step += 1
                    dve.wait_ge(half_done, step)
                    dve.scalar_tensor_tensor(out, xi[:, ct, :, j:j + NS], conv_w[:, ct, j:j + 1], out,
                                             ALU.mult, ALU.add).then_inc(
                                                 half_done if j < DCONV - 1 else conv_done, 1)
            for ct in range(CT):
                dve.wait_ge(conv_tanh, ct + 1)
                dve.tensor_scalar(delta[:, ct, :], delta[:, ct, :], 0.5, 0.5, ALU.mult, ALU.add).then_inc(half_done, 1)
                step += 1
                dve.wait_ge(half_done, step)
                dve.tensor_tensor(xc[:, ct, :], xc[:, ct, :], delta[:, ct, :], ALU.mult).then_inc(xc_done, 1)
            dve.wait_ge(a_exp, 1)
            dve.tensor_scalar(a_neg[:, :, :], a_neg[:, :, :], -1.0, None, ALU.mult).then_inc(a_ready, 1)
            for ct in range(CT):
                dve.wait_ge(soft, 3 * ct + 3)
                dve.scalar_tensor_tensor(delta[:, ct, :], delta[:, ct, :], 0.0, drive[ct % 2][:, :],
                                         ALU.max, ALU.add).then_inc(delta_done, 1)
            for r in range(1, 2 * DS, 2):
                for h in range(2):
                    dve.wait_ge(spread, 2 * r + h + 1)
                    i = dve.tensor_copy(bc[:, r, h * HT:(h + 1) * HT], banks[2 * (r % 4) + h][:, 0:HT])
                i.then_inc(bc_stored_v, 1)
            dve.wait_ge(bc_stored_a, DS)
            dve.wait_ge(bc_stored_v, DS)

            def finish(ct):
                dve.wait_ge(summed, DS * (ct + 1))
                for h in range(2):
                    at = slice(h * HT, (h + 1) * HT)
                    dve.scalar_tensor_tensor(xc[:, ct, at], xc[:, ct, at], skip[:, ct:ct + 1],
                                             banks[2 * (ct % 2) + h][:, 0:HT], ALU.mult, ALU.add).then_inc(skipped, 1)
                dve.wait_ge(skipped, 2 * ct + 2)
                dve.scalar_tensor_tensor(xc[:, ct, :], xc[:, ct, :], 0.5,
                                         z_gate[:, ct, :, :].rearrange("p b t -> p (b t)"),
                                         ALU.mult, ALU.mult).then_inc(gated, 1)

            for n in range(CT * DS):
                ct, s = n // DS, n % DS
                dve.wait_ge(decay_done, n + 1)
                dve.wait_ge(drive_done, n + 1)
                dve.tensor_tensor_scan(state[n % 2][:, :], decay[n % 2][:, :, :].rearrange("p b t -> p (b t)"),
                                       drive[n % 2][:, :], 0.0, ALU.mult, ALU.add).then_inc(scanned, 1)
                dve.wait_ge(scanned, n + 1)
                dve.tensor_tensor(drive[n % 2][:, :], state[n % 2][:, :], bc[:, DS + s, :],
                                  ALU.mult).then_inc(read_out, 1)
                if s == 2 and ct > 0:
                    finish(ct - 1)
            finish(CT - 1)
            for b in range(B):
                dve.wait_ge(out_projected, 2 * b + 1)
                dve.tensor_copy(mixed[:, b, 0, :], banks[4 + 2 * (b % 2)][:, 0:D]).then_inc(mixed_done, 1)
                dve.wait_ge(out_projected, 2 * b + 2)
                dve.tensor_copy(mixed[0:NS - P, b, 1, :], banks[5 + 2 * (b % 2)][0:NS - P, 0:D]).then_inc(mixed_done, 1)
            for t in range(TT):
                dve.wait_ge(scattered, t + 1)
                dve.tensor_tensor(X1[:, t, :], X1[:, t, :], banks[t % 4][:, 0:D], ALU.add).then_inc(added, 1)

        @block.tensor
        def _(pe):
            pe.wait_ge(loaded, 16 * LOADS)
            for ct in range(CT):
                pe.wait_ge(xc_done, ct + 1)
                for h in range(2):
                    i = pe.matmul(banks[h][0:RANK, 0:HT], xproj_w[:, ct, :], xc[:, ct, h * HT:(h + 1) * HT],
                                  start=(ct == 0), stop=(ct == CT - 1))
            i.then_inc(projected, 1)
            pe.wait_ge(proj_stored, 2)
            for ct in range(CT):
                for h in range(2):
                    n = 2 * ct + h
                    if n >= 4:
                        pe.wait_ge(dt_biased, n - 3)
                    pe.matmul(banks[2 + n % 4][:, 0:HT], dt_w[:, ct * P:(ct + 1) * P],
                              proj[0:DTR, h * HT:(h + 1) * HT], start=True, stop=True).then_inc(dt_projected, 1)
            pe.wait_ge(dt_biased, 2 * CT)
            for r in range(2 * DS):
                if r >= 4:
                    pe.wait_ge((bc_stored_a, bc_stored_v)[r % 2], (r - 4) // 2 + 1)
                for h in range(2):
                    pe.matmul(banks[2 * (r % 4) + h][:, 0:HT],
                              ident[0:RANK, DTR + r:DTR + r + 1].broadcast_to([RANK, P]),
                              proj[:, h * HT:(h + 1) * HT], start=True, stop=True).then_inc(spread, 1)
            pe.wait_ge(bc_stored_a, DS)
            pe.wait_ge(bc_stored_v, DS)
            for n in range(CT * DS):
                ct, s = n // DS, n % DS
                if s == 0 and ct >= 2:
                    pe.wait_ge(gated, ct - 1)
                pe.wait_ge(read_out, n + 1)
                for h in range(2):
                    i = pe.matmul(banks[2 * (ct % 2) + h][:, 0:HT], ident[:, :],
                                  drive[n % 2][:, h * HT:(h + 1) * HT], start=(s == 0), stop=(s == DS - 1))
                i.then_inc(summed, 1)
            pe.wait_ge(gated, CT)
            for b in range(B):
                for a in range(2):
                    if b >= 2:
                        pe.wait_ge(mixed_done, 2 * (b - 2) + a + 1)
                    m = P if a == 0 else NS - P
                    for ct in range(CT):
                        i = pe.matmul(banks[4 + 2 * (b % 2) + a][0:m, 0:D],
                                      xc[:, ct, b * NS + a * P:b * NS + a * P + m], out_w[:, ct, :],
                                      start=(ct == 0), stop=(ct == CT - 1))
                    i.then_inc(out_projected, 1)
            for t in range(TT):
                b = t // QT
                pe.wait_ge(mixed_done, 2 * b + 2)
                if t >= 4:
                    pe.wait_ge(added, t - 3)
                for a in range(2):
                    i = pe.matmul(banks[t % 4][:, 0:D], perm_T[:, b, a, (t % QT) * P:(t % QT + 1) * P],
                                  mixed[:, b, a, :], start=(a == 0), stop=(a == 1))
                i.then_inc(scattered, 1)


def experts(nc, w, X1, out, ident, banks):
    ctx = ExitStack()
    with ctx:
        def sb(name, shape, dt=F32):
            return ctx.enter_context(nc.sbuf_tensor(f"ex_{name}", shape, dt))

        def sem(name):
            return ctx.enter_context(nc.semaphore(f"ex_{name}"))

        NTOK = B * N1
        HALF = NTOK // 2
        router = sb("router", [P, DC, E])
        raw = sb("raw", [P, 3, DC, HID])
        w_hi = [sb(f"w_hi{i}", [P, 3, DC, HID], F32R) for i in range(2)]
        w_lo = [sb(f"w_lo{i}", [P, 3, DC, HID], F32R) for i in range(2)]
        one = sb("one", [P, 1])
        less = sb("less", [P, E, E])
        xf = sb("xf", [P, TT, D])
        xf_T = sb("xf_T", [P, DC, NTOK])
        x_hi = sb("x_hi", [P, DC, NTOK], F32R)
        x_lo = sb("x_lo", [P, DC, NTOK], F32R)
        logits = sb("logits", [P, TT, E])
        top = sb("top", [P, TT])
        p = sb("p", [P, TT, E])
        same = sb("same", [P, TT, E, E])
        above = sb("above", [P, TT, E, E])
        rank = sb("rank", [P, TT, E])
        chosen = sb("chosen", [P, TT, E])
        csum = sb("csum", [P, TT])
        combine = sb("combine", [P, TT, E])
        tanh = sb("tanh", [P, 2, HALF])
        gated = sb("gated", [P, 2, HALF])
        hidden = sb("hidden", [P, 2, HALF])
        h_hi = sb("h_hi", [P, HC2, NTOK], F32R)
        h_lo = sb("h_lo", [P, HC2, NTOK], F32R)
        norm = Norm(sb, sem, "norm", TT)

        router_loaded = sem("router_loaded")
        raw_loaded = sem("raw_loaded")
        consts = sem("consts")
        masked = sem("masked")
        w_hi_done = sem("w_hi_done")
        w_split = sem("w_split")
        transposed = sem("transposed")
        xf_T_stored = sem("xf_T_stored")
        x_hi_done = sem("x_hi_done")
        x_split = sem("x_split")
        logits_ready = sem("logits_ready")
        step = sem("step")
        p_exp = sem("p_exp")
        combine_ready = sem("combine_ready")
        gate_ready = sem("gate_ready")
        tanh_done = sem("tanh_done")
        gated_done = sem("gated_done")
        hidden_done = sem("hidden_done")
        h_hi_done = sem("h_hi_done")
        h_split = sem("h_split")
        down_done = sem("down_done")
        added = sem("added")
        stored = sem("stored")

        GU = 2 * HC2
        block = ctx.enter_context(nc.Block())

        @block.sync
        def _(sp):
            sp.dma_start(router[:, :, :], w["router_w"].rearrange("(c p) e -> p c e", p=P)).then_inc(router_loaded, 16)

            def load(e):
                for kind, name in enumerate(("w_gate", "w_up")):
                    sp.dma_start(raw[:, kind, :, :], w[name][bass.ds(e, 1), :, :].rearrange(
                        "o (c p) h -> p (o c) h", p=P)).then_inc(raw_loaded, 16)
                sp.dma_start(raw[:, 2, :, :].rearrange("p a n -> p (a n)").rearrange("p (c d) -> p c d", d=D),
                             w["w_down"][bass.ds(e, 1), :, :].rearrange(
                                 "o (c p) d -> p (o c) d", p=P)).then_inc(raw_loaded, 16)

            load(0)
            with sp.Fori(1, E) as e:
                sp.wait_ge(w_split, e)
                load(e)
            sp.wait_ge(added, E * TT + OPEN)
            sp.dma_start(out.rearrange("b (t p) d -> p (b t) d", p=P), X1[:, :, :]).then_inc(stored, 16)
            sp.wait_ge(stored, 16)

        @block.gpsimd
        def _(pool):
            pool.memset(one[:, :], 1.0).then_inc(consts, 1)
            pool.memset(less[:, :, :], 1.0).then_inc(consts, 1)
            pool.wait_ge(consts, 2)
            pool.affine_select(out=less[:, :, :], in_=less[:, :, :], compare_op=ALU.is_gt, fill=0.0,
                               base=0, pattern=[[1, E], [-1, E]], channel_multiplier=0).then_inc(masked, 1)
            ones = one[:, :].unsqueeze(2).unsqueeze(3).broadcast_to([P, 3, DC, HID])

            def split_weights(i, e):
                pool.wait_ge(raw_loaded, e * 48 + 48)
                pool.tensor_tensor(w_hi[i][:, :, :, :], raw[:, :, :, :], ones, ALU.mult).then_inc(w_hi_done, 1)
                pool.wait_ge(w_hi_done, e + 1)
                pool.tensor_tensor(w_lo[i][:, :, :, :], raw[:, :, :, :], w_hi[i][:, :, :, :].bitcast(F32),
                                   ALU.subtract).then_inc(w_split, 1)

            split_weights(0, 0)
            split_weights(1, 1)

            def low_parts(e):
                pool.wait_ge(down_done, e * TT + OPEN)
                for n in range(GU):
                    half, c = n // HC2, n % HC2
                    at = slice(half * HALF, (half + 1) * HALF)
                    pool.wait_ge(h_hi_done, e * GU + n + 1)
                    pool.tensor_tensor(h_lo[:, c, at], hidden[:, n % 2, :], h_hi[:, c, at].bitcast(F32),
                                       ALU.subtract).then_inc(h_split, 1)

            with pool.Fori(0, E // 2 - 1) as i:
                for k in range(2):
                    low_parts(2 * i + k)
                    pool.wait_ge(down_done, (2 * i + k) * TT + TT + OPEN)
                    split_weights(k, 2 * i + k + 2)
            for e in (E - 2, E - 1):
                low_parts(e)

        @block.scalar
        def _(act):
            norm.root(act, 0)
            for t in range(TT):
                act.wait_ge(transposed, t + 1)
                nc.scalar.activation(xf_T[:, :, t * P:(t + 1) * P],
                                     banks[t][:, 0:DC * P].rearrange("p (c q) -> p c q", c=DC),
                                     ACT.Copy).then_inc(xf_T_stored, 1)
            act.wait_ge(step, 2)
            nc.scalar.activation(p[:, :, :], logits[:, :, :], ACT.Exp).then_inc(p_exp, 1)
            with act.Fori(0, E) as e:
                act.wait_ge(down_done, e * TT + OPEN)
                for n in range(GU):
                    half, c = n // HC2, n % HC2
                    at = slice(half * HALF, (half + 1) * HALF)
                    act.wait_ge(gate_ready, e * GU + n + 1)
                    if n >= 2:
                        act.wait_ge(gated_done, e * GU + n - 1)
                    nc.scalar.activation(tanh[:, n % 2, :], banks[2 * (n % 2)][:, :], ACT.Tanh,
                                         scale=0.5).then_inc(tanh_done, 1)
                    act.wait_ge(hidden_done, e * GU + n + 1 + OPEN)
                    nc.scalar.activation(h_hi[:, c, at], hidden[:, n % 2, :], ACT.Copy).then_inc(h_hi_done, 1)

        @block.vector
        def _(dve):
            for opened in (hidden_done, added):
                dve.sem_inc(opened, OPEN)
            norm.normalize(dve, 0, X1, xf)
            for t in range(TT):
                at = slice(t * P, (t + 1) * P)
                dve.wait_ge(xf_T_stored, t + 1)
                dve.tensor_copy(x_hi[:, :, at], xf_T[:, :, at]).then_inc(x_hi_done, 1)
                dve.wait_ge(x_hi_done, t + 1)
                dve.tensor_tensor(x_lo[:, :, at], xf_T[:, :, at], x_hi[:, :, at].bitcast(F32),
                                  ALU.subtract).then_inc(x_split, 1)
            dve.wait_ge(logits_ready, 1)
            scores = banks[7][:, 0:TT * E].rearrange("p (t e) -> p t e", t=TT)
            dve.tensor_reduce(top[:, :], scores, AX_X, ALU.max).then_inc(step, 1)
            dve.wait_ge(step, 1)
            dve.tensor_tensor(logits[:, :, :], scores, top[:, :].unsqueeze(2).broadcast_to([P, TT, E]),
                              ALU.subtract).then_inc(step, 1)
            dve.wait_ge(p_exp, 1)
            dve.wait_ge(masked, 1)
            of_f = p[:, :, :].unsqueeze(2).broadcast_to([P, TT, E, E])
            of_e = p[:, :, :].unsqueeze(3).broadcast_to([P, TT, E, E])
            dve.tensor_tensor(same[:, :, :, :], of_f, of_e, ALU.is_equal).then_inc(step, 1)
            dve.tensor_tensor(above[:, :, :, :], of_f, of_e, ALU.is_gt).then_inc(step, 1)
            dve.wait_ge(step, 4)
            dve.tensor_tensor(same[:, :, :, :], same[:, :, :, :],
                              less[:, :, :].unsqueeze(1).broadcast_to([P, TT, E, E]), ALU.mult).then_inc(step, 1)
            dve.wait_ge(step, 5)
            dve.tensor_tensor(above[:, :, :, :], above[:, :, :, :], same[:, :, :, :], ALU.add).then_inc(step, 1)
            dve.wait_ge(step, 6)
            dve.tensor_reduce(rank[:, :, :], above[:, :, :, :], AX_X, ALU.add).then_inc(step, 1)
            dve.wait_ge(step, 7)
            dve.tensor_scalar(chosen[:, :, :], rank[:, :, :], float(K_TOP), None, ALU.is_lt).then_inc(step, 1)
            dve.wait_ge(step, 8)
            dve.tensor_tensor(chosen[:, :, :], chosen[:, :, :], p[:, :, :], ALU.mult).then_inc(step, 1)
            dve.wait_ge(step, 9)
            dve.tensor_reduce(csum[:, :], chosen[:, :, :], AX_X, ALU.add).then_inc(step, 1)
            dve.wait_ge(step, 10)
            dve.reciprocal(top[:, :], csum[:, :]).then_inc(step, 1)
            dve.wait_ge(step, 11)
            dve.scalar_tensor_tensor(combine[:, :, :], chosen[:, :, :], 0.5,
                                     top[:, :].unsqueeze(2).broadcast_to([P, TT, E]),
                                     ALU.mult, ALU.mult).then_inc(combine_ready, 1)
            dve.wait_ge(combine_ready, 1)

            def pieces(e, half):
                for c in range(HC2):
                    n = half * HC2 + c
                    b = 2 * (n % 2)
                    dve.wait_ge(tanh_done, e * GU + n + 1)
                    dve.scalar_tensor_tensor(gated[:, n % 2, :], tanh[:, n % 2, :], 1.0, banks[b][:, :],
                                             ALU.add, ALU.mult).then_inc(gated_done, 1)
                    dve.wait_ge(gated_done, e * GU + n + 1)
                    if n >= 2:
                        dve.wait_ge(h_split, e * GU + n - 1)
                    dve.tensor_tensor(hidden[:, n % 2, :], gated[:, n % 2, :], banks[b + 1][:, :],
                                      ALU.mult).then_inc(hidden_done, 1)

            def add(e, half):
                for t in range(half * TT // 2, (half + 1) * TT // 2):
                    dve.wait_ge(down_done, e * TT + t + 1 + OPEN)
                    dve.scalar_tensor_tensor(X1[:, t, :], banks[4 + t % 4][:, 0:D],
                                             combine[:, t, bass.ds(e, 1)], X1[:, t, :],
                                             ALU.mult, ALU.add).then_inc(added, 1)

            with dve.Fori(0, E) as e:
                pieces(e, 0)
                pieces(e, 1)
                add(e, 0)
                add(e, 1)

        @block.tensor
        def _(pe):
            pe.sem_inc(down_done, OPEN)
            for t in range(TT):
                pe.wait_ge(norm.done, norm.tiles_done(0, t + 1))
                for c in range(DC):
                    i = pe.transpose(banks[t][:, c * P:(c + 1) * P], xf[:, t, c * P:(c + 1) * P], ident[:, :])
                i.then_inc(transposed, 1)
            pe.wait_ge(router_loaded, 16)
            pe.wait_ge(xf_T_stored, TT)
            for t in range(TT):
                for c in range(DC):
                    i = pe.matmul(banks[7][:, t * E:(t + 1) * E], xf_T[:, c, t * P:(t + 1) * P],
                                  router[:, c, :], start=(c == 0), stop=(c == DC - 1))
            i.then_inc(logits_ready, 1)
            pe.wait_ge(x_split, TT)

            def up(k, e, half):
                for c in range(HC2):
                    n = half * HC2 + c
                    b = 2 * (n % 2)
                    at = slice(half * HALF, (half + 1) * HALF)
                    if n >= 2:
                        pe.wait_ge(hidden_done, e * GU + n - 1 + OPEN)
                    for kind in range(2):
                        for d in range(DC):
                            wh, wl = (x[k][:, kind, d, c * P:(c + 1) * P] for x in (w_hi, w_lo))
                            pe.matmul(banks[b + kind][:, :], wh, x_hi[:, d, at], start=(d == 0), stop=False)
                            pe.matmul(banks[b + kind][:, :], wh, x_lo[:, d, at], start=False, stop=False)
                            i = pe.matmul(banks[b + kind][:, :], wl, x_hi[:, d, at], start=False,
                                          stop=(d == DC - 1))
                    i.then_inc(gate_ready, 1)

            def down(k, e, half):
                for t in range(half * TT // 2, (half + 1) * TT // 2):
                    if t == half * TT // 2:
                        pe.wait_ge(h_split, e * GU + (half + 1) * HC2)
                    if t >= 4:
                        pe.wait_ge(added, e * TT + t - 3 + OPEN)
                    for c in range(HC2):
                        hh, hl = (x[:, c, t * P:(t + 1) * P] for x in (h_hi, h_lo))
                        wh, wl = (x[k][:, 2, :, :].rearrange("p a n -> p (a n)")[:, c * D:(c + 1) * D]
                                  for x in (w_hi, w_lo))
                        o = banks[4 + t % 4][:, 0:D]
                        pe.matmul(o, hh, wh, start=(c == 0), stop=False)
                        pe.matmul(o, hh, wl, start=False, stop=False)
                        i = pe.matmul(o, hl, wh, start=False, stop=(c == HC2 - 1))
                    i.then_inc(down_done, 1)

            pe.wait_ge(combine_ready, 1)
            with pe.Fori(0, E // 2) as i:
                for k in range(2):
                    e = 2 * i + k
                    pe.wait_ge(w_split, e + 1)
                    pe.wait_ge(hidden_done, e * GU + OPEN)
                    up(k, e, 0)
                    up(k, e, 1)
                    pe.wait_ge(added, e * TT + OPEN)
                    down(k, e, 0)
                    down(k, e, 1)


def program(nc, x, ctxT, xattn, attn, ffn, out):
    ctx = ExitStack()
    with ctx:
        X1 = ctx.enter_context(nc.sbuf_tensor("X1", [P, TT, D], F32))
        ident = ctx.enter_context(nc.sbuf_tensor("ident", [P, P], F32))
        banks = [ctx.enter_context(nc.psum_tensor(f"bank{i}", [P, 512], F32)) for i in range(8)]
        cross_attention(nc, x, ctxT, xattn, X1, ident, banks)
        with ExitStack() as mixer:
            def sb(name, shape):
                return mixer.enter_context(nc.sbuf_tensor(name, shape, F32))

            perm_T = sb("perm_T", [P, B, 2, N1])
            mixed = sb("mixed", [P, B, 2, D])
            xi = sb("xi", [P, CT, B, NS + DCONV - 1])
            z_gate = sb("z_gate", [P, CT, B, NS])
            route_and_project(nc, attn, X1, perm_T, xi, z_gate, mixed, ident, banks)
            state_space(nc, attn, X1, perm_T, xi, z_gate, mixed, ident, banks)
        experts(nc, ffn, X1, out, ident, banks)


def kernel(**inputs):
    import concourse.bacc as _bacc
    from concourse.bass_utils import run_bass_kernel_spmd as _run

    nc = _bacc.Bacc("TRN2", target_bir_lowering=False, num_devices=1)
    arrays = {}

    def give(name, a):
        a = np.ascontiguousarray(a)
        arrays[f"in_{name}_dram"] = a
        return nc.dram_tensor(f"in_{name}_dram", a.shape, mybir.dt.from_np(a.dtype), kind="ExternalInput").ap()

    x = give("x", inputs["x"])
    ctxT = give("ctxT", np.asarray(inputs["ctx_1024"]).transpose(0, 2, 1))
    xattn, attn, ffn = {}, {}, {}
    for name, a in inputs.items():
        a = np.asarray(a)
        if name.startswith("L0_xattn_"):
            xattn[name[9:]] = give(name, a)
        elif name.startswith("L0_attn_"):
            if name[8:] in ("bq", "bk", "conv_b", "dt_b", "Dp"):
                a = a.reshape(-1, P).T
            attn[name[8:]] = give(name, a)
        elif name == "L0_ffn_router_w":
            ffn["router_w"] = give(name, a.T)
        elif name.startswith("L0_ffn_"):
            ffn[name[7:]] = give(name, a.transpose(0, 2, 1))
    out = nc.dram_tensor("out_0_dram", (B, N1, D), F32, kind="ExternalOutput").ap()
    program(nc, x, ctxT, xattn, attn, ffn, out)
    r = _run(nc, [arrays], core_ids=[0])
    return r.results[0]["out_0_dram"]
```

```python
from contextlib import ExitStack
import numpy as np
import concourse.bass as bass
from concourse import mybir

F32 = mybir.dt.float32
F32R = mybir.dt.float32r
ALU = mybir.AluOpType
ACT = mybir.ActivationFunctionType
AX_X = mybir.AxisListType.X

P = 128
B, N1, D = 4, 256, 256
N2 = 4096
DC = D // P
QT = N1 // P
TT = B * QT
HEADS, HD = 8, 64
INNER = HEADS * HD
IC = INNER // P
PAIRS = IC
KG = 512
NG = 1 + N2 // KG
KT = (N1 + N2) // P

AH, AHD = 16, 16
TOP = N1 // 4
NS = N1 - TOP
HC = P // AHD
RH = D // 2
DIN = 2 * D
CT = DIN // P
DS, DCONV = 16, 4
DTR = D // 16
RANK = DTR + 2 * DS
GELU = 0.7978845608028654

E, K_TOP, HID = 8, 2, 512
HC2 = HID // P
EPS = 1e-5
OPEN = 1
LAG = 3
CHUNKS = N2 // KG
AHEAD = 2
RING = 3


def by_dve(kt):
    return kt % 4 == 2


def summed(by, kt):
    return sum(by_dve(t) == by for t in range(kt + 1))


def group_keys(g):
    return (0, N1) if g == 0 else (N1 + (g - 1) * KG, KG)


class Norm:

    STEPS = 6

    def __init__(self, sb, sem, name, n):
        self.n = n
        self.stats = sb(f"{name}_stats", [P, n, 6])
        self.agg = sb(f"{name}_agg", [P, n, 2])
        self.var = sb(f"{name}_var", [P, n])
        self.root_var = sb(f"{name}_root_var", [P, n])
        self.guess = sb(f"{name}_guess", [P, n])
        self.square = sb(f"{name}_square", [P, n])
        self.factor = sb(f"{name}_factor", [P, n])
        self.rstd = sb(f"{name}_rstd", [P, n])
        self.done = sem(f"{name}_done")
        self.root_done = sem(f"{name}_root_done")
        self.per_call = 3 * n + self.STEPS

    def normalize(self, dve, calls, x, out):
        n, done = self.n, self.done
        at = calls * self.per_call
        for t in range(n):
            dve.bn_stats(self.stats[:, t, :], x[:, t, :]).then_inc(done, 1)
        dve.wait_ge(done, at + n)
        for t in range(n):
            dve.bn_aggr(self.agg[:, t, :], self.stats[:, t, :]).then_inc(done, 1)
        dve.wait_ge(done, at + 2 * n)
        dve.tensor_scalar(self.var[:, :], self.agg[:, :, 1], EPS, None, ALU.add).then_inc(done, 1)
        dve.wait_ge(self.root_done, calls + 1)
        dve.reciprocal(self.guess[:, :], self.root_var[:, :]).then_inc(done, 1)
        dve.wait_ge(done, at + 2 * n + 2)
        dve.tensor_tensor(self.square[:, :], self.guess[:, :], self.guess[:, :], ALU.mult).then_inc(done, 1)
        dve.wait_ge(done, at + 2 * n + 3)
        dve.scalar_tensor_tensor(self.factor[:, :], self.square[:, :], -0.5, self.var[:, :], ALU.mult,
                                 ALU.mult).then_inc(done, 1)
        dve.wait_ge(done, at + 2 * n + 4)
        dve.scalar_tensor_tensor(self.rstd[:, :], self.factor[:, :], 1.5, self.guess[:, :], ALU.add,
                                 ALU.mult).then_inc(done, 2)
        dve.wait_ge(done, at + 2 * n + 6)
        for t in range(n):
            dve.tensor_scalar(out[:, t, :], x[:, t, :], self.agg[:, t, 0:1], self.rstd[:, t:t + 1],
                              ALU.subtract, ALU.mult).then_inc(done, 1)

    def root(self, act, calls):
        act.wait_ge(self.done, calls * self.per_call + 2 * self.n + 1)
        act.activation(self.root_var[:, :], self.var[:, :], ACT.Sqrt).then_inc(self.root_done, 1)

    def tiles_done(self, calls, tiles):
        return calls * self.per_call + 2 * self.n + self.STEPS + tiles


def cross_attention(nc, x, ctxT, w, X1, ident, banks):
    wq, wk1, wv1, wk2, wv2, wo, bo = (w[n] for n in ("Wq1", "Wk1", "Wv1", "Wk2", "Wv2", "Wo", "bo"))
    ctx, sems = ExitStack(), []
    with ctx:
        def sb(name, shape, dt=F32):
            return ctx.enter_context(nc.sbuf_tensor(name, shape, dt))

        def sem(name):
            sems.append(ctx.enter_context(nc.semaphore(name)))
            return sems[-1]

        ones = sb("xa_ones", [P, P], F32R)
        one = sb("xa_one", [P, 1])
        ctx_hi = sb("xa_ctx_hi", [P, DC, N2], F32R)
        with nc.sbuf_tensor("xa_ctx_in", [P, DC, N2], F32) as ctx_in:
            pass
        ctx_lo = sb("xa_ctx_lo", [P, DC, N2], F32R)
        with nc.sbuf_tensor("xa_xl_T", [P, DC, B * N1], F32) as xl_T:
            pass
        own_lo = sb("xa_own_lo", [P, DC, B * N1], F32R)
        own_hi = sb("xa_own_hi", [P, DC, N1], F32R)
        w_raw = sb("xa_w_raw", [P, 5, DC, P])
        w_hi = sb("xa_w_hi", [P, 4, DC, P], F32R)
        w_lo = sb("xa_w_lo", [P, 4, DC, P], F32R)
        q_w_hi = sb("xa_q_w_hi", [P, DC, 2, 2, HD], F32R)
        q_w_lo = sb("xa_q_w_lo", [P, DC, 2, 2, HD], F32R)
        q_hi = sb("xa_q_hi", [P, 2, N1], F32R)
        q_lo = sb("xa_q_lo", [P, 2, N1], F32R)
        with nc.sbuf_tensor("xa_xl", [P, TT, D], F32) as xl:
            pass
        keys = [sb(f"xa_keys{h}", [P, KT * P], F32R) for h in range(2)]
        vals = sb("xa_vals", [P, KT, 2, 2, HD], F32R)
        maxes = sb("xa_maxes", [P, 4, NG])
        rowmax = sb("xa_rowmax", [P, 4])
        neg_diag = sb("xa_neg_diag", [P, 2, N1], F32R)
        probs = sb("xa_probs", [P, RING, 2 * N1])
        probs_hi = sb("xa_probs_hi", [P, RING, 2 * N1], F32R)
        probs_lo = sb("xa_probs_lo", [P, RING, 2 * N1], F32R)
        prob_sums = [sb(f"xa_prob_sums{i}", [P, 2 * N1]) for i in range(2)]
        vals_raw = sb("xa_vals_raw", [P, KG])
        o_low, inv_sum = vals_raw[:, 0:N1], vals_raw[:, N1:2 * N1]
        o_sum = sb("xa_o_sum", [P, N1])
        heads_T = sb("xa_heads_T", [P, IC, N1])
        wo_sb = sb("xa_wo", [P, IC, D])
        bo_sb = heads_T[:, 0, :]

        x_loaded = sem("xa_x_loaded")
        norm = Norm(sb, sem, "xa_norm", TT)
        setup = sem("xa_setup")
        ident_ready = sem("xa_ident_ready")
        xl_transposed = sem("xa_xl_transposed")
        xl_T_stored = sem("xa_xl_T_stored")
        own_hi_done = sem("xa_own_hi_done")
        own_split = sem("xa_own_split")
        ctx_loaded = [sem(f"xa_ctx_loaded{c}") for c in range(CHUNKS)]
        ctx_hi_done = sem("xa_ctx_hi_done")
        ctx_split = sem("xa_ctx_split")
        w_loaded = sem("xa_w_loaded")
        w_hi_done = sem("xa_w_hi_done")
        w_split = sem("xa_w_split")
        q_projected = sem("xa_q_projected")
        q_hi_done = sem("xa_q_hi_done")
        q_split = sem("xa_q_split")
        k_projected = sem("xa_k_projected")
        k_hi_done = sem("xa_k_hi_done")
        k_split = sem("xa_k_split")
        v_projected = sem("xa_v_projected")
        vt_stored = sem("xa_vt_stored")
        v_transposed = sem("xa_v_transposed")
        v_stored = sem("xa_v_stored")
        v_split = sem("xa_v_split")
        max_scored = sem("xa_max_scored")
        max_reduced = sem("xa_max_reduced")
        rowmax_done = sem("xa_rowmax_done")
        diag_ready = sem("xa_diag_ready")
        scores_ready = sem("xa_scores_ready")
        exp_done = sem("xa_exp_done")
        probs_hi_done = sem("xa_probs_hi_done")
        probs_split = sem("xa_probs_split")
        probs_summed = sem("xa_probs_summed")
        dve_summed = sem("xa_dve_summed")
        pv_done = sem("xa_pv_done")
        sums_ready = sem("xa_sums_ready")
        o_low_taken = sem("xa_o_low_taken")
        o_taken = sem("xa_o_taken")
        sums_inverted = sem("xa_sums_inverted")
        o_normalized = sem("xa_o_normalized")
        out_projected = sem("xa_out_projected")
        x1_done = sem("xa_x1_done")

        k_bank = banks[0:2]
        s_bank = banks[2:6]
        o_bank = banks[6:8]

        w_pieces = [(w_raw[:, 1 + k, :, :], w_hi[:, k, :, :], w_lo[:, k, :, :]) for k in range(4)]
        w_pieces += [(w_raw[:, 0, :, :].rearrange("p c (h e) -> p c h e", h=2), q_w_hi[:, :, :, dup, :],
                      q_w_lo[:, :, :, dup, :]) for dup in range(2)]
        W_PARTS = len(w_pieces)

        block = ctx.enter_context(nc.Block())

        @block.sync
        def _(sp):
            sp.dma_start(X1[:, :, :], x.rearrange("b (t p) d -> p (b t) d", p=P)).then_inc(x_loaded, 16)
            sp.dma_start(bo_sb, bo.rearrange("(a d) -> a d", a=1).broadcast_to([P, D])).then_inc(x_loaded, 16)
            sp.dma_start(wo_sb[:, :, :], wo.rearrange("(c p) n -> p c n", p=P)).then_inc(x_loaded, 16)

            def load_pair(pair):
                for kind, w in enumerate((wq, wk1, wk2, wv1, wv2)):
                    sp.dma_start(w_raw[:, kind, :, :],
                                 w.rearrange("(c p) n -> p c n", p=P)[:, :, bass.ds(pair * P, P)]
                                 ).then_inc(w_loaded, 16)

            load_pair(0)

            def load_chunk(b, c):
                sp.dma_start(ctx_in[:, :, c * KG:(c + 1) * KG],
                             ctxT[bass.ds(b, 1), :, c * KG:(c + 1) * KG].rearrange(
                                 "o (c p) n -> p (o c) n", p=P)).then_inc(ctx_loaded[c], 16)

            def load_pairs(b):
                with sp.Fori(0, PAIRS) as p:
                    sp.wait_ge(w_split, (b * PAIRS + p) * W_PARTS + W_PARTS)
                    load_pair((p + 1) % PAIRS)

            for c in range(CHUNKS):
                load_chunk(0, c)
            with sp.Fori(0, B - 1) as b:
                load_pairs(b)
                for c in range(CHUNKS):
                    sp.wait_ge(v_projected, b * (PAIRS * NG) + (PAIRS - 1) * NG + c + 2 + OPEN)
                    load_chunk(b + 1, c)
            load_pairs(B - 1)
            sp.wait_ge(w_loaded, 5 * 16 * (B * PAIRS + 1))

        @block.gpsimd
        def _(pool):
            for opened in (ctx_split, v_split, probs_summed):
                pool.sem_inc(opened, OPEN)
            pool.memset(ident[:, :], 0.0).then_inc(setup, 1)
            pool.memset(ones[:, :].bitcast(F32), 1.0).then_inc(setup, 1)
            pool.memset(one[:, :], 1.0).then_inc(setup, 1)
            pool.wait_ge(setup, 3)
            pool.affine_select(out=ident[:, :], in_=ident[:, :], compare_op=ALU.not_equal, fill=1.0,
                               base=0, pattern=[[-1, P]], channel_multiplier=1).then_inc(ident_ready, 1)

            def split_chunk(b, c):
                at = slice(c * KG, (c + 1) * KG)
                pool.wait_ge(ctx_hi_done, b * CHUNKS + c + 1)
                pool.tensor_tensor(ctx_lo[:, :, at], ctx_in[:, :, at],
                                   ctx_hi[:, :, at].bitcast(F32), ALU.subtract).then_inc(ctx_split, 1)

            def do_pair(b, u, first):
                if first:
                    for c in range(AHEAD):
                        split_chunk(b, c)
                def split_values(g):
                    k0, n = group_keys(g)
                    raw = vals_raw[:, 0:n].rearrange("p (t h e) -> p t h e", h=2, e=HD)
                    hi, lo = (vals[:, k0 // P:(k0 + n) // P, :, part, :] for part in range(2))
                    pool.wait_ge(v_stored, u * NG + g + 1)
                    pool.tensor_tensor(lo, raw, hi.bitcast(F32), ALU.subtract).then_inc(v_split, 1)

                for g in range(NG):
                    if first and g + AHEAD < CHUNKS:
                        split_chunk(b, g + AHEAD)
                    if g >= 1:
                        split_values(g - 1)
                split_values(NG - 1)
                for kt in range(KT):
                    if by_dve(kt):
                        continue
                    total, new = prob_sums[0][:, :], probs[:, kt % RING, :]
                    pool.wait_ge(exp_done, u * KT + kt + 1 + OPEN)
                    if kt == 0:
                        pool.wait_ge(sums_ready, u + OPEN)
                        pool.tensor_tensor(total, new, one[:, :].broadcast_to([P, 2 * N1]),
                                           ALU.mult).then_inc(probs_summed, 1)
                    else:
                        pool.wait_ge(probs_summed, u * summed(False, KT - 1) + summed(False, kt) - 1 + OPEN)
                        pool.tensor_tensor(total, total, new, ALU.add).then_inc(probs_summed, 1)

            with pool.Fori(0, B) as b:
                do_pair(b, b * PAIRS, True)
                with pool.Fori(1, PAIRS) as p:
                    do_pair(b, b * PAIRS + p, False)

        @block.scalar
        def _(act):
            act.sem_inc(exp_done, OPEN)
            norm.root(act, 0)

            def split_weights(done, k):
                raw, hi, _ = w_pieces[k]
                nc.scalar.activation(hi, raw, ACT.Copy).then_inc(w_hi_done, 1)

            def split_chunk(b, c):
                at = slice(c * KG, (c + 1) * KG)
                act.wait_ge(ctx_loaded[c], b * 16 + 16)
                nc.scalar.activation(ctx_hi[:, :, at], ctx_in[:, :, at], ACT.Copy
                                     ).then_inc(ctx_hi_done, 1)

            def do_pair(b, u, first):
                if first:
                    for c in range(AHEAD):
                        split_chunk(b, c)

                def store_values(g):
                    k0, n = group_keys(g)
                    act.wait_ge(v_transposed, u * NG + g + 1)
                    act.wait_ge(v_split, u * NG + g + OPEN)
                    if g == 0:
                        act.wait_ge(o_normalized, u + OPEN)
                    nc.scalar.activation(vals[:, k0 // P:(k0 + n) // P, :, 0, :],
                                         o_bank[1][:, 0:n].rearrange("p (t h e) -> p t h e", h=2, e=HD), ACT.Copy)
                    nc.scalar.activation(vals_raw[:, 0:n], o_bank[1][:, 0:n], ACT.Copy
                                         ).then_inc(v_stored, 1)

                for g in range(NG):
                    k0, n = group_keys(g)
                    act.wait_ge(k_projected, u * NG + g + 1)
                    nc.scalar.activation(keys[0][0:HD, k0:k0 + n], k_bank[g % 2][0:HD, 0:n],
                                         ACT.Copy).then_inc(k_hi_done, 1)
                    nc.scalar.activation(keys[1][HD:P, k0:k0 + n], k_bank[g % 2][HD:P, 0:n],
                                         ACT.Copy).then_inc(k_hi_done, 1)
                    if g == 0:
                        act.wait_ge(probs_summed, u * summed(False, KT - 1) + OPEN)
                    if g == NG - 1:
                        store_values(g - 1)
                    act.wait_ge(v_projected, u * NG + g + 1 + OPEN)
                    if g >= 2:
                        act.wait_ge(v_transposed, u * NG + g - 1)
                    nc.scalar.activation(probs[:, g % 2, 0:n], o_bank[0][:, 0:n], ACT.Copy
                                         ).then_inc(vt_stored, 1)
                    if 1 <= g < NG - 1:
                        store_values(g - 1)
                    if first and g + AHEAD < CHUNKS:
                        split_chunk(b, g + AHEAD)
                store_values(NG - 1)
                for kt in range(KT):
                    act.wait_ge(scores_ready, u * KT + kt + 1)
                    if kt >= RING:
                        t = kt - RING
                        act.wait_ge(probs_split, u * KT + t + 1)
                        if by_dve(t):
                            act.wait_ge(dve_summed, u * summed(True, KT - 1) + summed(True, t))
                        else:
                            act.wait_ge(probs_summed, u * summed(False, KT - 1) + summed(False, t) + OPEN)
                    if kt % 2 == 0:
                        if kt >= RING:
                            act.wait_ge(pv_done, u * KT + kt - RING + 1 + OPEN)
                        nc.scalar.activation(probs_hi[:, kt % RING, :], s_bank[kt % 4][:, :], ACT.Exp,
                                             scale=HD ** -0.5)
                    nc.scalar.activation(probs[:, kt % RING, :], s_bank[kt % 4][:, :], ACT.Exp,
                                         scale=HD ** -0.5).then_inc(exp_done, 1)
                    if kt % 2 == 1 and kt // 2 < W_PARTS:
                        if kt == 1:
                            act.wait_ge(w_loaded, (u + 2) * (5 * 16))
                        split_weights(u + 1, kt // 2)
                act.wait_ge(pv_done, u * KT + KT + OPEN)
                for h in range(2):
                    nc.scalar.activation(o_low[h * HD:(h + 1) * HD, :], o_bank[h][HD:P, 0:N1], ACT.Copy
                                         ).then_inc(o_low_taken, 1)

            act.wait_ge(w_loaded, 5 * 16)
            for k in range(W_PARTS):
                split_weights(0, k)
            act.wait_ge(xl_transposed, TT)
            with act.Fori(0, B) as b:
                do_pair(b, b * PAIRS, True)
                with act.Fori(1, PAIRS) as p:
                    do_pair(b, b * PAIRS + p, False)

        @block.vector
        def _(dve):
            for opened in (o_taken, sums_inverted, o_normalized):
                dve.sem_inc(opened, OPEN)
            dve.wait_ge(x_loaded, 48)
            norm.normalize(dve, 0, X1, xl)
            for t in range(TT):
                dve.tensor_tensor(X1[:, t, :], X1[:, t, :], bo_sb, ALU.add).then_inc(x1_done, 1)
            for t in range(TT):
                dve.wait_ge(xl_transposed, t + 1)
                src = s_bank[t % 4][:, 0:DC * P].rearrange("p (c q) -> p c q", c=DC)
                dve.tensor_copy(xl_T[:, :, t * P:(t + 1) * P], src).then_inc(xl_T_stored, 1)

            def split_weights(done, k):
                raw, hi, lo = w_pieces[k]
                dve.wait_ge(w_hi_done, done * W_PARTS + k + 1)
                dve.tensor_tensor(lo, raw, hi.bitcast(F32), ALU.subtract).then_inc(w_split, 1)

            def do_pair(b, p, u):
                dve.wait_ge(q_projected, u + 1)
                q_ps = s_bank[0][:, :].rearrange("p (h q) -> p h q", h=2)
                dve.tensor_copy(q_hi[:, :, :], q_ps).then_inc(q_hi_done, 1)
                dve.wait_ge(q_hi_done, u + 1)
                dve.tensor_tensor(q_lo[:, :, :], q_ps, q_hi[:, :, :].bitcast(F32),
                                  ALU.subtract).then_inc(q_split, 1)

                def reduce_max(g):
                    for h in range(2):
                        n = group_keys(g)[1]
                        dve.wait_ge(max_scored, u * (2 * NG) + 2 * g + h + 1)
                        for qt in range(QT):
                            i = dve.tensor_reduce(maxes[:, 2 * h + qt, g:g + 1],
                                                  s_bank[2 * h + qt][:, 0:n], AX_X, ALU.max)
                        i.then_inc(max_reduced, 1)

                for g in range(NG):
                    k0, n = group_keys(g)
                    for h in range(2):
                        hi, lo = (slice(0, HD), slice(HD, P)) if h == 0 else (slice(HD, P), slice(0, HD))
                        dve.wait_ge(k_hi_done, u * (2 * NG) + 2 * g + h + 1)
                        i = dve.tensor_tensor(keys[h][lo, k0:k0 + n], k_bank[g % 2][hi, 0:n],
                                              keys[h][hi, k0:k0 + n].bitcast(F32), ALU.subtract)
                    i.then_inc(k_split, 1)
                    if g >= 1:
                        reduce_max(g - 1)
                reduce_max(NG - 1)
                dve.wait_ge(max_reduced, u * (2 * NG) + 2 * NG)
                dve.tensor_reduce(rowmax[:, :], maxes[:, :, :], AX_X, ALU.max).then_inc(rowmax_done, 1)
                dve.wait_ge(rowmax_done, u + 1)
                for h in range(2):
                    for qt in range(QT):
                        j = 2 * h + qt
                        dve.tensor_scalar(neg_diag[:, h, qt * P:(qt + 1) * P], ident[:, :],
                                          rowmax[:, j:j + 1], -1.0, ALU.mult,
                                          ALU.mult).then_inc(diag_ready, 1)
                for kt in range(KT):
                    new, hi, lo = probs[:, kt % RING, :], probs_hi[:, kt % RING, :], probs_lo[:, kt % RING, :]
                    dve.wait_ge(exp_done, u * KT + kt + 1 + OPEN)
                    if kt >= RING:
                        dve.wait_ge(pv_done, u * KT + kt - RING + 1 + OPEN)
                    if kt % 2 == 1:
                        dve.tensor_copy(hi, new).then_inc(probs_hi_done, 1)
                        dve.wait_ge(probs_hi_done, u * (KT // 2) + kt // 2 + 1)
                    dve.tensor_tensor(lo, new, hi.bitcast(F32), ALU.subtract).then_inc(probs_split, 1)
                    if by_dve(kt):
                        total = prob_sums[1][:, :]
                        if summed(True, kt) == 1:
                            dve.tensor_copy(total, new).then_inc(dve_summed, 1)
                        else:
                            dve.wait_ge(dve_summed, u * summed(True, KT - 1) + summed(True, kt) - 1)
                            dve.tensor_tensor(total, total, new, ALU.add).then_inc(dve_summed, 1)
                    if kt % 2 == 0 and 1 <= kt // 2 <= W_PARTS:
                        split_weights(u + 1, kt // 2 - 1)
                for h in range(2):
                    dve.wait_ge(o_low_taken, u * 2 + h + 1)
                    at = slice(h * HD, (h + 1) * HD)
                    dve.tensor_tensor(o_sum[at, :], o_bank[h][0:HD, 0:N1], o_low[at, :],
                                      ALU.add).then_inc(o_taken, 1)
                dve.wait_ge(sums_ready, u + 1 + OPEN)
                dve.reciprocal(inv_sum, k_bank[1][:, 0:N1]).then_inc(sums_inverted, 1)
                dve.wait_ge(sums_inverted, u + 1 + OPEN)
                dve.wait_ge(out_projected, b * QT + OPEN)
                dve.tensor_tensor(heads_T[:, p, :], o_sum[:, :].unsqueeze(1),
                                  inv_sum.unsqueeze(1), ALU.mult).then_inc(o_normalized, 1)

            for k in range(W_PARTS):
                split_weights(0, k)
            with dve.Fori(0, B) as b:
                latents = bass.ds(b * N1, N1)
                dve.tensor_copy(own_hi[:, :, :], xl_T[:, :, latents]).then_inc(own_hi_done, 1)
                dve.wait_ge(own_hi_done, b + 1)
                dve.tensor_tensor(own_lo[:, :, latents], xl_T[:, :, latents], own_hi[:, :, :].bitcast(F32),
                                  ALU.subtract).then_inc(own_split, 1)
                do_pair(b, bass.ds(0, 1), b * PAIRS)
                with dve.Fori(1, PAIRS) as p:
                    do_pair(b, bass.ds(p, 1), b * PAIRS + p)
                for qt in range(QT):
                    dve.wait_ge(out_projected, b * QT + qt + 1 + OPEN)
                    at = bass.ds(b * QT + qt, 1)
                    dve.tensor_tensor(X1[:, at, :], k_bank[qt][:, 0:D].rearrange("p (o d) -> p o d", o=1),
                                      X1[:, at, :], ALU.add).then_inc(x1_done, 1)

        @block.tensor
        def _(pe):
            for opened in (pv_done, v_projected, sums_ready, out_projected):
                pe.sem_inc(opened, OPEN)
            pe.wait_ge(ident_ready, 1)
            for t in range(TT):
                pe.wait_ge(norm.done, norm.tiles_done(0, t + 1))
                if t >= 4:
                    pe.wait_ge(xl_T_stored, t - 3)
                for c in range(DC):
                    i = pe.transpose(s_bank[t % 4][:, c * P:(c + 1) * P], xl[:, t, c * P:(c + 1) * P], ident[:, :])
                i.then_inc(xl_transposed, 1)
            pe.wait_ge(xl_T_stored, TT)

            def product3(out, lhs, rhs, first=True, last=True):
                n = len(lhs)
                for c in range(n):
                    (lh, ll), (rh, rl) = lhs[c], rhs[c]
                    for k, (l, r) in enumerate(((lh, rh), (lh, rl), (ll, rh))):
                        i = pe.matmul(out, l, r, start=(c == 0 and k == 0), stop=(c == n - 1 and k == 2))
                return i

            def do_pair(b, u, first):
                pe.wait_ge(w_split, u * W_PARTS + W_PARTS)
                if first:
                    pe.wait_ge(own_split, b + 1)
                pe.wait_ge(exp_done, u * KT + OPEN)

                def chunks(g):
                    if g == 0:
                        return [(own_hi[:, c, :], own_lo[:, c, bass.ds(b * N1, N1)]) for c in range(DC)]
                    at = slice((g - 1) * KG, g * KG)
                    return [(ctx_hi[:, c, at], ctx_lo[:, c, at]) for c in range(DC)]

                def project_keys(g):
                    n = group_keys(g)[1]
                    kind = 0 if g == 0 else 1
                    if g == 0 and first:
                        pe.wait_ge(x1_done, b * QT + TT)
                    elif g == 1:
                        pe.wait_ge(sums_inverted, u + OPEN)
                    if g >= 1 and first:
                        pe.wait_ge(ctx_split, b * CHUNKS + g + OPEN)
                    if g >= 2:
                        pe.wait_ge(k_split, u * NG + g - 1)
                    product3(k_bank[g % 2][:, 0:n],
                             [(w_hi[:, kind, c, :], w_lo[:, kind, c, :]) for c in range(DC)],
                             chunks(g)).then_inc(k_projected, 1)

                def project_values(g):
                    n = group_keys(g)[1]
                    kind = 2 if g == 0 else 3
                    if g == 0:
                        pe.wait_ge(o_taken, u * 2 + OPEN)
                    else:
                        pe.wait_ge(vt_stored, u * NG + g)
                    product3(o_bank[0][:, 0:n],
                             [(w_hi[:, kind, c, :], w_lo[:, kind, c, :]) for c in range(DC)],
                             chunks(g)).then_inc(v_projected, 1)

                def turn_values(g):
                    n = group_keys(g)[1]
                    pe.wait_ge(vt_stored, u * NG + g + 1)
                    if g >= 1:
                        pe.wait_ge(v_stored, u * NG + g)
                    for t in range(n // P):
                        at = slice(t * P, (t + 1) * P)
                        i = pe.transpose(o_bank[1][:, at], probs[:, g % 2, at], ident[:, :])
                    i.then_inc(v_transposed, 1)

                def score_for_max(g):
                    k0, n = group_keys(g)
                    pe.wait_ge(k_split, u * NG + g + 1)
                    if g == 0:
                        pe.wait_ge(q_split, u + 1)
                    for h in range(2):
                        if g >= 1:
                            pe.wait_ge(max_reduced, u * (2 * NG) + 2 * g - 1 + h)
                        for qt in range(QT):
                            i = pe.matmul(s_bank[2 * h + qt][:, 0:n], q_hi[:, h, qt * P:(qt + 1) * P],
                                          keys[h][:, k0:k0 + n], start=True, stop=True)
                        i.then_inc(max_scored, 1)

                for h in range(2):
                    i = product3(s_bank[0][:, h * N1:(h + 1) * N1],
                                 [(q_w_hi[:, c, h, :, :].rearrange("p a e -> p (a e)"),
                                   q_w_lo[:, c, h, :, :].rearrange("p a e -> p (a e)")) for c in range(DC)],
                                 [(own_hi[:, c, :], own_lo[:, c, bass.ds(b * N1, N1)]) for c in range(DC)])
                i.then_inc(q_projected, 1)
                for g in range(NG):
                    project_keys(g)
                    if g < NG - 1:
                        project_values(g)
                    if g >= 1:
                        score_for_max(g - 1)
                        turn_values(g - 1)
                score_for_max(NG - 1)
                project_values(NG - 1)
                turn_values(NG - 1)

                pe.wait_ge(diag_ready, u * 4 + 4)
                for kt in range(KT + LAG):
                    if kt < KT:
                        if kt >= 4:
                            pe.wait_ge(exp_done, u * KT + kt - 3 + OPEN)
                        at = slice(kt * P, (kt + 1) * P)
                        for h in range(2):
                            out = s_bank[kt % 4][:, h * N1:(h + 1) * N1]
                            pe.matmul(out, keys[h][:, at], q_hi[:, h, :], start=True, stop=False)
                            pe.matmul(out, keys[h][:, at], q_lo[:, h, :], start=False, stop=False)
                            i = pe.matmul(out, ones[:, :], neg_diag[:, h, :], start=False, stop=True)
                        i.then_inc(scores_ready, 1)
                    if kt >= LAG:
                        t = kt - LAG
                        if t == 0:
                            pe.wait_ge(v_split, u * NG + NG + OPEN)
                        pe.wait_ge(probs_split, u * KT + t + 1)
                        for h in range(2):
                            out = o_bank[h][:, 0:N1]
                            v = vals[:, t, h, :, :].rearrange("p a e -> p (a e)")
                            pe.matmul(out, v, probs_hi[:, t % RING, h * N1:(h + 1) * N1],
                                      start=(t == 0), stop=False)
                            i = pe.matmul(out, v, probs_lo[:, t % RING, h * N1:(h + 1) * N1],
                                          start=False, stop=(t == KT - 1))
                        i.then_inc(pv_done, 1)
                for j in (1, 0):
                    if j == 1:
                        pe.wait_ge(dve_summed, (u + 1) * summed(True, KT - 1))
                    else:
                        pe.wait_ge(probs_summed, (u + 1) * summed(False, KT - 1) + OPEN)
                    for h in range(2):
                        i = pe.matmul(k_bank[1][h * HD:(h + 1) * HD, 0:N1], ones[:, 0:HD].bitcast(F32),
                                      prob_sums[j][:, h * N1:(h + 1) * N1], start=(j == 1), stop=(j == 0))
                i.then_inc(sums_ready, 1)

            with pe.Fori(0, B) as b:
                do_pair(b, b * PAIRS, True)
                with pe.Fori(1, PAIRS) as p:
                    do_pair(b, b * PAIRS + p, False)
                pe.wait_ge(o_normalized, (b + 1) * PAIRS + OPEN)
                for qt in range(QT):
                    for c in range(IC):
                        i = pe.matmul(k_bank[qt][:, 0:D], heads_T[:, c, qt * P:(qt + 1) * P], wo_sb[:, c, :],
                                      start=(c == 0), stop=(c == IC - 1))
                    i.then_inc(out_projected, 1)

    with nc.Block() as block:
        @block.gpsimd
        def _(pool):
            for used in sems:
                pool.sem_clear(used)


def route_and_project(nc, w, X1, perm_T, xi, z_gate, mixed, ident, banks):
    ctx = ExitStack()
    with ctx:
        def sb(name, shape, dt=F32):
            return ctx.enter_context(nc.sbuf_tensor(f"mx_{name}", shape, dt))

        def sem(name):
            return ctx.enter_context(nc.semaphore(f"mx_{name}"))

        lnw = sb("lnw", [P, D])
        lnb = sb("lnb", [P, D])
        rw1 = sb("rw1", [P, DC, RH])
        rb1 = sb("rb1", [P, 1])
        rw2 = sb("rw2", [P, 1])
        rb2 = sb("rb2", [P, 1])
        wq = sb("wq", [P, DC, D])
        wk = sb("wk", [P, DC, D])
        wv = sb("wv", [P, DC, D])
        wo = sb("wo", [P, DC, D])
        bq = sb("bq", [P, DC])
        bk = sb("bk", [P, DC])
        bv = sb("bv", [P, D])
        bo = sb("bo", [P, D])
        in_w = sb("in_w", [P, DC, 2 * DIN])
        y = sb("y", [P, TT, D])
        xn = sb("xn", [P, TT, D])
        xn_T = sb("xn_T", [P, DC, B * N1])
        z = sb("z", [P, B * N1])
        z2 = sb("z2", [P, B * N1])
        th = sb("th", [P, B * N1])
        rw2_bc = sb("rw2_bc", [P, P])
        score = sb("score", [P, B * N1])
        own = sb("own", [P, TT, P])
        score_col = sb("score_col", [P, TT])
        above = sb("above", [P, TT, N1])
        ties = sb("ties", [P, TT, N1])
        rank = sb("rank", [P, TT])
        other = sb("other", [P, TT])
        base = sb("base", [P, TT])
        diff = sb("diff", [P, TT])
        diff2 = sb("diff2", [P, TT])
        place = sb("place", [P, TT])
        ones = sb("ones", [P, P])
        before = sb("before", [P, P])
        earlier = sb("earlier", [P, QT, N1])
        columns = sb("columns", [P, N1])
        perm = sb("perm", [P, TT, N1])
        xp = sb("xp", [P, DC, B, N1])
        xa = sb("xa", [P, DC, B, 2, TOP])
        q_T = sb("q_T", [P, DC, B, 2 * TOP])
        k_T = sb("k_T", [P, DC, B, TOP])
        head_mask = sb("head_mask", [P, HC])
        pair_mask = sb("pair_mask", [P, D // 2 // AHD, 2, AHD])
        k_heads = sb("k_heads", [P, DC, HC, TOP])
        k_heads2 = sb("k_heads2", [P, DC, HC, TOP])
        v_biased = sb("v_biased", [P, 2, D])
        v2 = sb("v2", [P, B, D])
        top = sb("top", [P, B, AH])
        e = sb("e", [P, 2, AH, TOP])
        esum = sb("esum", [P, B, AH])
        rsum = sb("rsum", [P, B, AH])
        probs = sb("probs", [P, 2, AH, TOP])
        probs_T = sb("probs_T", [P, 2, AH // 2, P])
        o = sb("o", [P, 2, D])
        o_T = sb("o_T", [P, 2, DC, P])
        zt = sb("zt", [P, 2, 2 * NS])
        norm = Norm(sb, sem, "norm", TT)

        loaded = sem("loaded")
        consts = sem("consts")
        masked = sem("masked")
        columns_ready = sem("columns_ready")
        rw2_ready = sem("rw2_ready")
        x1_added = sem("x1_added")
        weighted = sem("weighted")
        xn_ready = sem("xn_ready")
        xn_transposed = sem("xn_transposed")
        xn_T_stored = sem("xn_T_stored")
        hidden = sem("hidden")
        z_stored = sem("z_stored")
        gelu_in = sem("gelu_in")
        tanh_done = sem("tanh_done")
        gelu_done = sem("gelu_done")
        scored = sem("scored")
        score_stored = sem("score_stored")
        own_done = sem("own_done")
        score_col_done = sem("score_col_done")
        ties_done = sem("ties_done")
        above_done = sem("above_done")
        rank_done = sem("rank_done")
        other_done = sem("other_done")
        counted = sem("counted")
        place_step = sem("place_step")
        perm_done = sem("perm_done")
        perm_transposed = sem("perm_transposed")
        perm_T_stored = sem("perm_T_stored")
        permuted = sem("permuted")
        xp_stored = sem("xp_stored")
        xa_stored = sem("xa_stored")
        qk_projected = sem("qk_projected")
        qk_stored = sem("qk_stored")
        v_projected = sem("v_projected")
        v_biased_done = sem("v_biased_done")
        v2_done = sem("v2_done")
        inner_projected = sem("inner_projected")
        xi_stored = sem("xi_stored")
        z_tanh = sem("z_tanh")
        z_done = sem("z_done")
        k_heads_done = sem("k_heads_done")
        a_scored = sem("a_scored")
        top_done = sem("top_done")
        shifted = sem("shifted")
        exp_done = sem("exp_done")
        esum_done = sem("esum_done")
        rsum_done = sem("rsum_done")
        probs_done = sem("probs_done")
        probs_transposed = sem("probs_transposed")
        probs_T_stored = sem("probs_T_stored")
        o_ready = sem("o_ready")
        o_stored = sem("o_stored")
        o_transposed = sem("o_transposed")
        o_T_stored = sem("o_T_stored")
        a_out = sem("a_out")
        mixed_done = sem("mixed_done")

        block = ctx.enter_context(nc.Block())

        @block.sync
        def _(sp):
            def row(v):
                return v.rearrange("(a d) -> a d", a=1).broadcast_to([P, v.shape[0]])

            chunks = "(c p) n -> p c n"
            for dst, src in ((lnw[:, :], row(w["ln_w"])), (lnb[:, :], row(w["ln_b"])),
                             (rw1[:, :, :], w["r_w1"].rearrange(chunks, p=P)),
                             (rb1[:, :], w["r_b1"].rearrange("(p a) -> p a", a=1)), (rw2[:, :], w["r_w2"]),
                             (rb2[:, :], row(w["r_b2"])),
                             (wq[:, :, :], w["Wq"].rearrange(chunks, p=P)),
                             (wk[:, :, :], w["Wk"].rearrange(chunks, p=P)),
                             (wv[:, :, :], w["Wv"].rearrange(chunks, p=P)),
                             (wo[:, :, :], w["Wo"].rearrange(chunks, p=P)),
                             (bq[:, :], w["bq"]),
                             (bk[:, :], w["bk"]),
                             (bv[:, :], row(w["bv"])), (bo[:, :], row(w["bo"])),
                             (in_w[:, :, :], w["in_w"].rearrange(chunks, p=P))):
                sp.dma_start(dst, src).then_inc(loaded, 16)

        LOADS = 15

        @block.gpsimd
        def _(pool):
            pool.memset(ones[:, :], 1.0).then_inc(consts, 1)
            pool.memset(before[:, :], 1.0).then_inc(consts, 1)
            pool.memset(earlier[:, :, :], 1.0).then_inc(consts, 1)
            pool.memset(head_mask[:, :], 1.0).then_inc(consts, 1)
            pool.memset(pair_mask[:, :, :, :], 1.0).then_inc(consts, 1)
            pool.memset(xi[:, :, :, 0:DCONV - 1], 0.0).then_inc(consts, 1)
            pool.iota(columns[:, :], pattern=[[1, N1]], base=0, channel_multiplier=0,
                      allow_small_or_imprecise_dtypes=True).then_inc(columns_ready, 1)
            pool.wait_ge(consts, 6)
            pool.affine_select(out=before[:, :], in_=before[:, :], compare_op=ALU.is_gt, fill=0.0,
                               base=0, pattern=[[1, P]], channel_multiplier=-1).then_inc(masked, 1)
            pool.affine_select(out=earlier[:, :, :], in_=earlier[:, :, :], compare_op=ALU.is_gt, fill=0.0,
                               base=0, pattern=[[P, QT], [-1, N1]], channel_multiplier=1).then_inc(masked, 1)
            pool.affine_select(out=head_mask[:, :], in_=head_mask[:, :], compare_op=ALU.is_ge, fill=0.0,
                               base=0, pattern=[[-AHD, HC]], channel_multiplier=1).then_inc(masked, 1)
            for h, (op, at) in enumerate(((ALU.is_ge, TOP - 1), (ALU.is_ge, -TOP))):
                part = pair_mask[:, :, h, :]
                pool.affine_select(out=part, in_=part, compare_op=op, fill=0.0, base=at,
                                   pattern=[[0, D // 2 // AHD], [0, AHD]],
                                   channel_multiplier=-1 if h == 0 else 1).then_inc(masked, 1)
            pool.wait_ge(masked, 3)
            pool.affine_select(out=head_mask[:, :], in_=head_mask[:, :], compare_op=ALU.is_ge, fill=0.0,
                               base=AHD - 1, pattern=[[AHD, HC]], channel_multiplier=-1).then_inc(masked, 1)
            pool.wait_ge(norm.done, norm.tiles_done(0, TT))
            pool.tensor_tensor(X1[:, :, :], X1[:, :, :], y[:, :, :], ALU.add).then_inc(x1_added, 1)
            for b in range(B):
                pool.wait_ge(xp_stored, b + 1)
                for dup in range(2):
                    pool.tensor_copy(xa[:, :, b, dup, :], xp[:, :, b, NS:N1]).then_inc(xa_stored, 1)
            pool.wait_ge(masked, 6)
            for b in range(B):
                kh = (k_heads, k_heads2)[b % 2]
                pool.wait_ge(qk_stored, 2 * DC)
                if b >= 2:
                    pool.wait_ge(a_scored, b - 1)
                for c in range(DC):
                    pool.tensor_tensor(kh[:, c, :, :],
                                       k_T[:, c, b, :].unsqueeze(1).broadcast_to([P, HC, TOP]),
                                       head_mask[:, :].unsqueeze(2).broadcast_to([P, HC, TOP]),
                                       ALU.mult).then_inc(k_heads_done, 1)

        @block.scalar
        def _(act):
            norm.root(act, 0)
            norm.root(act, 1)
            for t in range(TT):
                act.wait_ge(xn_transposed, t + 1)
                nc.scalar.activation(xn_T[:, :, t * P:(t + 1) * P],
                                     banks[t][:, 0:DC * P].rearrange("p (c q) -> p c q", c=DC),
                                     ACT.Copy).then_inc(xn_T_stored, 1)
            act.wait_ge(loaded, 16 * LOADS)
            for n in range(2):
                act.wait_ge(hidden, n + 1)
                nc.scalar.activation(z[:, n * 512:(n + 1) * 512], banks[n][:, :], ACT.Identity,
                                     bias=rb1[:, 0:1]).then_inc(z_stored, 1)
            act.wait_ge(gelu_in, 1)
            nc.scalar.activation(th[:, :], z2[:, :], ACT.Tanh, scale=GELU).then_inc(tanh_done, 1)
            for b in range(B):
                act.wait_ge(perm_transposed, b + 1)
                nc.scalar.activation(perm_T[:, b, :, :], banks[4 + b][:, :].rearrange(
                    "p (a t) -> p a t", a=2), ACT.Copy).then_inc(perm_T_stored, 1)
            for c in range(DC):
                act.wait_ge(qk_projected, 2 * c + 1)
                nc.scalar.activation(q_T[:, c, :, :], banks[2 * c][:, :].rearrange("p (b q) -> p b q", b=B),
                                     ACT.Identity, bias=bq[:, c:c + 1]).then_inc(qk_stored, 1)
                act.wait_ge(qk_projected, 2 * c + 2)
                nc.scalar.activation(k_T[:, c, :, :], banks[2 * c + 1][:, 0:B * TOP].rearrange(
                    "p (b q) -> p b q", b=B), ACT.Identity, bias=bk[:, c:c + 1]).then_inc(qk_stored, 1)
            for n in range(2 * CT * 2):
                ct, half = n // 2, n % 2
                act.wait_ge(inner_projected, n + 1)
                bank = banks[n % 4][:, 0:2 * NS]
                if ct < CT:
                    nc.scalar.activation(xi[:, ct, 2 * half:2 * half + 2, DCONV - 1:],
                                         bank.rearrange("p (b t) -> p b t", b=2), ACT.Copy).then_inc(xi_stored, 1)
                else:
                    m = n - 2 * CT
                    if m >= 2:
                        act.wait_ge(z_done, m - 1)
                    nc.scalar.activation(zt[:, m % 2, :], bank, ACT.Tanh, scale=0.5).then_inc(z_tanh, 1)
            for b in range(B):
                act.wait_ge(shifted, b + 1)
                nc.scalar.activation(e[:, b % 2, :, :], e[:, b % 2, :, :], ACT.Exp,
                                     scale=AHD ** -0.5).then_inc(exp_done, 1)
                if b >= 2:
                    act.wait_ge(o_ready, b - 1)
                for n in range(2):
                    act.wait_ge(probs_transposed, 2 * b + n + 1)
                    nc.scalar.activation(probs_T[:, b % 2, 4 * n:4 * n + 4, :],
                                         banks[4 + n][:, :].rearrange("p (a q) -> p a q", a=4),
                                         ACT.Copy).then_inc(probs_T_stored, 1)
                act.wait_ge(o_ready, b + 1)
                nc.scalar.activation(o[:, b % 2, :], banks[6][:, 0:D], ACT.Copy).then_inc(o_stored, 1)
                act.wait_ge(o_transposed, b + 1)
                nc.scalar.activation(o_T[:, b % 2, :, :], banks[7][:, 0:DC * P].rearrange(
                    "p (c q) -> p c q", c=DC), ACT.Copy).then_inc(o_T_stored, 1)

        @block.vector
        def _(dve):
            norm.normalize(dve, 0, X1, y)
            dve.wait_ge(norm.done, norm.tiles_done(0, TT))
            norm.normalize(dve, 1, y, xn)
            dve.wait_ge(norm.done, norm.tiles_done(1, TT))
            dve.wait_ge(loaded, 16 * LOADS)
            dve.tensor_tensor(xn[:, :, :], xn[:, :, :], lnw[:, :].unsqueeze(1).broadcast_to([P, TT, D]),
                              ALU.mult).then_inc(weighted, 1)
            dve.wait_ge(weighted, 1)
            for t in range(TT):
                dve.tensor_tensor(xn[:, t, :], xn[:, t, :], lnb[:, :], ALU.add).then_inc(xn_ready, 1)
            dve.wait_ge(consts, 6)
            dve.tensor_scalar(rw2_bc[:, :], ones[:, :], rw2[:, 0:1], None, ALU.mult).then_inc(rw2_ready, 1)
            dve.wait_ge(z_stored, 2)
            dve.tensor_tensor(z2[:, :], z[:, :], z[:, :], ALU.mult).then_inc(place_step, 1)
            dve.wait_ge(place_step, 1)
            dve.tensor_scalar(z2[:, :], z2[:, :], 0.044715, 1.0, ALU.mult, ALU.add).then_inc(place_step, 1)
            dve.wait_ge(place_step, 2)
            dve.tensor_tensor(z2[:, :], z2[:, :], z[:, :], ALU.mult).then_inc(gelu_in, 1)
            dve.wait_ge(tanh_done, 1)
            dve.scalar_tensor_tensor(z[:, :], th[:, :], 1.0, z[:, :], ALU.add, ALU.mult).then_inc(gelu_done, 1)
            for n in range(2):
                dve.wait_ge(scored, n + 1)
                dve.tensor_scalar(score[:, n * 512:(n + 1) * 512], banks[2 + n][:, :], 0.5, rb2[:, 0:1],
                                  ALU.mult, ALU.add).then_inc(score_stored, 1)
            dve.wait_ge(score_stored, 2)
            dve.tensor_tensor(own[:, :, :], score[:, :].rearrange("p (t j) -> p t j", t=TT),
                              ident[:, :].unsqueeze(1).broadcast_to([P, TT, P]), ALU.mult).then_inc(own_done, 1)
            dve.wait_ge(own_done, 1)
            dve.tensor_reduce(score_col[:, :], own[:, :, :], AX_X, ALU.add).then_inc(score_col_done, 1)
            dve.wait_ge(score_col_done, 1)
            dve.wait_ge(masked, 6)
            for t in range(TT):
                all_scores = score[:, (t // QT) * N1:(t // QT + 1) * N1]
                dve.scalar_tensor_tensor(ties[:, t, :], all_scores, score_col[:, t:t + 1],
                                         earlier[:, t % QT, :], ALU.is_equal, ALU.mult).then_inc(ties_done, 1)
            for t in range(TT):
                all_scores = score[:, (t // QT) * N1:(t // QT + 1) * N1]
                dve.wait_ge(ties_done, t + 1)
                dve.scalar_tensor_tensor(above[:, t, :], all_scores, score_col[:, t:t + 1],
                                         ties[:, t, :], ALU.is_gt, ALU.add).then_inc(above_done, 1)
            dve.wait_ge(above_done, TT)
            dve.tensor_reduce(rank[:, :], above[:, :, :], AX_X, ALU.add).then_inc(rank_done, 1)
            dve.wait_ge(rank_done, 1)
            dve.tensor_scalar(other[:, :], rank[:, :], float(TOP), None, ALU.is_ge).then_inc(other_done, 1)
            dve.tensor_scalar(base[:, :], rank[:, :], float(NS), None, ALU.add).then_inc(place_step, 1)
            dve.wait_ge(counted, 1)
            dve.wait_ge(place_step, 3)
            dve.tensor_tensor(diff[:, :].rearrange("p (b t) -> p t b", t=QT),
                              banks[0][:, 0:TT].rearrange("p (t b) -> p t b", t=QT),
                              base[:, :].rearrange("p (b t) -> p t b", t=QT), ALU.subtract).then_inc(place_step, 1)
            dve.wait_ge(place_step, 4)
            dve.wait_ge(other_done, 1)
            dve.tensor_tensor(diff2[:, :], diff[:, :], other[:, :], ALU.mult).then_inc(place_step, 1)
            dve.wait_ge(place_step, 5)
            dve.tensor_tensor(place[:, :], diff2[:, :], base[:, :], ALU.add).then_inc(place_step, 1)
            dve.wait_ge(place_step, 6)
            dve.wait_ge(columns_ready, 1)
            for t in range(TT):
                dve.tensor_scalar(perm[:, t, :], columns[:, :], place[:, t:t + 1], None,
                                  ALU.is_equal).then_inc(perm_done, 1)
            for b in range(B):
                dve.wait_ge(permuted, b + 1)
                dve.tensor_copy(xp[:, :, b, :], banks[b][:, :].rearrange("p (c q) -> p c q", c=DC)
                                ).then_inc(xp_stored, 1)
            for b in range(B):
                dve.wait_ge(v_projected, b + 1)
                if b >= 2:
                    dve.wait_ge(v2_done, b - 1)
                dve.tensor_tensor(v_biased[:, b % 2, :], banks[4 + b % 2][:, 0:D], bv[:, :],
                                  ALU.add).then_inc(v_biased_done, 1)
                dve.wait_ge(v_biased_done, b + 1)
                dve.tensor_tensor(v2[:, b, :], v_biased[:, b % 2, :],
                                  pair_mask[:, :, :, :].rearrange("p a h e -> p (a h e)"),
                                  ALU.mult).then_inc(v2_done, 1)
            for m in range(2 * CT):
                n = 2 * CT + m
                dve.wait_ge(z_tanh, m + 1)
                dve.scalar_tensor_tensor(
                    z_gate[:, m // 2, 2 * (m % 2):2 * (m % 2) + 2, :],
                    zt[:, m % 2, :].rearrange("p (b t) -> p b t", b=2), 1.0,
                    banks[n % 4][:, 0:2 * NS].rearrange("p (b t) -> p b t", b=2),
                    ALU.add, ALU.mult).then_inc(z_done, 1)
            for b in range(B):
                s = [banks[2 * (b % 2) + c][:, :].rearrange("p (h k) -> p h k", h=HC) for c in range(DC)]
                dve.wait_ge(a_scored, b + 1)
                for c in range(DC):
                    dve.tensor_reduce(top[:, b, c * HC:(c + 1) * HC], s[c], AX_X, ALU.max).then_inc(top_done, 1)
                if b >= 2:
                    dve.wait_ge(probs_done, b - 1)
                dve.wait_ge(top_done, 2 * b + 2)
                for c in range(DC):
                    i = dve.tensor_tensor(e[:, b % 2, c * HC:(c + 1) * HC, :], s[c],
                                          top[:, b, c * HC:(c + 1) * HC].unsqueeze(2).broadcast_to([P, HC, TOP]),
                                          ALU.subtract)
                i.then_inc(shifted, 1)
                dve.wait_ge(exp_done, b + 1)
                dve.tensor_reduce(esum[:, b, :], e[:, b % 2, :, :], AX_X, ALU.add).then_inc(esum_done, 1)
                dve.wait_ge(esum_done, b + 1)
                dve.reciprocal(rsum[:, b, :], esum[:, b, :]).then_inc(rsum_done, 1)
                dve.wait_ge(rsum_done, b + 1)
                if b >= 2:
                    dve.wait_ge(probs_transposed, 2 * b - 2)
                dve.tensor_tensor(probs[:, b % 2, :, :], e[:, b % 2, :, :],
                                  rsum[:, b, :].unsqueeze(2).broadcast_to([P, AH, TOP]),
                                  ALU.mult).then_inc(probs_done, 1)
                if b >= 1:
                    dve.wait_ge(a_out, b)
                    dve.tensor_tensor(mixed[TOP:P, b - 1, 1, :], banks[7][TOP:P, 0:D], bo[TOP:P, :],
                                      ALU.add).then_inc(mixed_done, 1)
            dve.wait_ge(a_out, B)
            dve.tensor_tensor(mixed[TOP:P, B - 1, 1, :], banks[7][TOP:P, 0:D], bo[TOP:P, :],
                              ALU.add).then_inc(mixed_done, 1)

        @block.tensor
        def _(pe):
            for t in range(TT):
                pe.wait_ge(xn_ready, t + 1)
                for c in range(DC):
                    i = pe.transpose(banks[t][:, c * P:(c + 1) * P], xn[:, t, c * P:(c + 1) * P], ident[:, :])
                i.then_inc(xn_transposed, 1)
            pe.wait_ge(loaded, 16 * LOADS)
            pe.wait_ge(xn_T_stored, TT)
            for n in range(2):
                for c in range(DC):
                    i = pe.matmul(banks[n][:, :], rw1[:, c, :], xn_T[:, c, n * 512:(n + 1) * 512],
                                  start=(c == 0), stop=(c == DC - 1))
                i.then_inc(hidden, 1)
            pe.wait_ge(rw2_ready, 1)
            pe.wait_ge(gelu_done, 1)
            for n in range(2):
                pe.matmul(banks[2 + n][:, :], rw2_bc[:, :], z[:, n * 512:(n + 1) * 512],
                          start=True, stop=True).then_inc(scored, 1)
            pe.wait_ge(other_done, 1)
            pe.wait_ge(consts, 6)
            pe.wait_ge(masked, 6)
            pe.wait_ge(z_stored, 2)
            o3 = other[:, :].rearrange("p (b t) -> p b t", t=QT)
            pe.matmul(banks[0][:, 0:B], before[:, :], o3[:, :, 0], start=True, stop=True)
            pe.matmul(banks[0][:, B:2 * B], ones[:, :], o3[:, :, 0], start=True, stop=False)
            pe.matmul(banks[0][:, B:2 * B], before[:, :], o3[:, :, 1], start=False, stop=True).then_inc(counted, 1)
            pe.wait_ge(place_step, 4)
            for b in range(B):
                pe.wait_ge(perm_done, QT * (b + 1))
                for c in range(DC):
                    for t in range(QT):
                        i = pe.matmul(banks[b][:, c * N1:(c + 1) * N1], xn[:, QT * b + t, c * P:(c + 1) * P],
                                      perm[:, QT * b + t, :], start=(t == 0), stop=(t == QT - 1))
                i.then_inc(permuted, 1)
                for a in range(2):
                    for t in range(QT):
                        i = pe.transpose(banks[4 + b][:, a * N1 + t * P:a * N1 + (t + 1) * P],
                                         perm[:, QT * b + t, a * P:(a + 1) * P], ident[:, :])
                i.then_inc(perm_transposed, 1)
            pe.wait_ge(xa_stored, 2 * B)
            for c in range(DC):
                for d in range(DC):
                    i = pe.matmul(banks[2 * c][:, :], wq[:, d, c * P:(c + 1) * P],
                                  xa[:, d, :, :, :].rearrange("p b a q -> p (b a q)"),
                                  start=(d == 0), stop=(d == DC - 1))
                i.then_inc(qk_projected, 1)
                for d in range(DC):
                    i = pe.matmul(banks[2 * c + 1][:, 0:B * TOP], wk[:, d, c * P:(c + 1) * P],
                                  xa[:, d, :, 0, :], start=(d == 0), stop=(d == DC - 1))
                i.then_inc(qk_projected, 1)
            pe.wait_ge(perm_T_stored, B)
            for b in range(B):
                if b >= 2:
                    pe.wait_ge(v_biased_done, b - 1)
                for d in range(DC):
                    i = pe.matmul(banks[4 + b % 2][:, 0:D], xa[:, d, b, :, :].rearrange("p a q -> p (a q)"),
                                  wv[:, d, :], start=(d == 0), stop=(d == DC - 1))
                i.then_inc(v_projected, 1)
            pe.wait_ge(qk_stored, 2 * DC)
            for n in range(2 * CT * 2):
                ct, half = n // 2, n % 2
                if 4 <= n < 2 * CT + 4:
                    pe.wait_ge(xi_stored, n - 3)
                elif n >= 2 * CT + 4:
                    pe.wait_ge(z_done, n - 3 - 2 * CT)
                for d in range(DC):
                    i = pe.matmul(banks[n % 4][:, 0:2 * NS], in_w[:, d, ct * P:(ct + 1) * P],
                                  xp[:, d, 2 * half:2 * half + 2, 0:NS], start=(d == 0), stop=(d == DC - 1))
                i.then_inc(inner_projected, 1)
            pe.wait_ge(z_done, 2 * CT)
            pe.wait_ge(v2_done, B)

            def attend_scores(b):
                pe.wait_ge(k_heads_done, DC * (b + 1))
                if b >= 2:
                    pe.wait_ge(shifted, b - 1)
                for c in range(DC):
                    i = pe.matmul(banks[2 * (b % 2) + c][:, :], q_T[:, c, b, :],
                                  (k_heads, k_heads2)[b % 2][:, c, :, :].rearrange("p h k -> p (h k)"),
                                  start=True, stop=True)
                i.then_inc(a_scored, 1)

            attend_scores(0)
            for b in range(B):
                if b + 1 < B:
                    attend_scores(b + 1)
                pe.wait_ge(probs_done, b + 1)
                flat = probs[:, b % 2, :, :].rearrange("p h k -> p (h k)")
                for n in range(2):
                    if b >= 1:
                        pe.wait_ge(probs_T_stored, 2 * b - 1 + n)
                    for a in range(4):
                        pair = 4 * n + a
                        i = pe.transpose(banks[4 + n][:, a * P:(a + 1) * P],
                                         flat[:, pair * P:(pair + 1) * P], ident[:, :])
                    i.then_inc(probs_transposed, 1)
                pe.wait_ge(probs_T_stored, 2 * b + 2)
                if b >= 1:
                    pe.wait_ge(o_stored, b)
                for pair in range(AH // 2):
                    i = pe.matmul(banks[6][:, pair * 2 * AHD:(pair + 1) * 2 * AHD], probs_T[:, b % 2, pair, :],
                                  v2[:, b, pair * 2 * AHD:(pair + 1) * 2 * AHD], start=True, stop=True)
                i.then_inc(o_ready, 1)
                pe.wait_ge(o_stored, b + 1)
                if b >= 1:
                    pe.wait_ge(mixed_done, b)
                for c in range(DC):
                    i = pe.transpose(banks[7][:, c * P:(c + 1) * P], o[:, b % 2, c * P:(c + 1) * P], ident[:, :])
                i.then_inc(o_transposed, 1)
                pe.wait_ge(o_T_stored, b + 1)
                for c in range(DC):
                    i = pe.matmul(banks[7][:, 0:D], o_T[:, b % 2, c, :], wo[:, c, :],
                                  start=(c == 0), stop=(c == DC - 1))
                i.then_inc(a_out, 1)


def state_space(nc, w, X1, perm_T, xi, z_gate, mixed, ident, banks):
    ctx = ExitStack()
    with ctx:
        def sb(name, shape, dt=F32):
            return ctx.enter_context(nc.sbuf_tensor(f"ss_{name}", shape, dt))

        def sem(name):
            return ctx.enter_context(nc.semaphore(f"ss_{name}"))

        NT = B * NS
        HT = NT // 2
        RINGS, DECAYS = 4, 3
        conv_w = sb("conv_w", [P, CT, DCONV])
        conv_b = sb("conv_b", [P, CT])
        xproj_w = sb("xproj_w", [P, CT, RANK])
        dt_w = sb("dt_w", [DTR, DIN])
        dt_b = sb("dt_b", [P, CT])
        a_log = sb("a_log", [P, CT, DS])
        a_neg = sb("a_neg", [P, CT, DS])
        skip = sb("skip", [P, CT])
        out_w = sb("out_w", [P, CT, D])
        xc = sb("xc", [P, CT, NT])
        delta = sb("delta", [P, CT, NT])
        proj = sb("proj", [RANK, NT])
        LOW = 64
        parts = sb("parts", [P, NT], F32R)
        pick = sb("pick", [P, RANK], F32R)
        bc = sb("bc", [P, 2 * DS, NT])
        decay = [sb(f"decay{i}", [P, B, NS]) for i in range(DECAYS)]
        drive = [sb(f"drive{i}", [P, NT]) for i in range(RINGS)]
        dx = xi[:, :, :, :].rearrange("p c b t -> p (c b t)")[:, 0:CT * NT].rearrange("p (c n) -> p c n", c=CT)

        loaded = sem("loaded")
        conv_done = sem("conv_done")
        conv_tanh = sem("conv_tanh")
        half_done = sem("half_done")
        xc_done = sem("xc_done")
        projected = sem("projected")
        proj_stored = sem("proj_stored")
        proj_hi_done = sem("proj_hi_done")
        proj_split = sem("proj_split")
        pick_ready = sem("pick_ready")
        blank = sem("blank")
        dt_projected = sem("dt_projected")
        dt_biased = sem("dt_biased")
        soft = sem("soft")
        delta_done = sem("delta_done")
        dx_done = sem("dx_done")
        a_exp = sem("a_exp")
        a_ready = sem("a_ready")
        spread = sem("spread")
        bc_stored_a = sem("bc_stored_a")
        bc_stored_v = sem("bc_stored_v")
        zeroed = sem("zeroed")
        decay_done = sem("decay_done")
        drive_done = sem("drive_done")
        scanned = sem("scanned")
        read_out = sem("read_out")
        summed = sem("summed")
        skipped = sem("skipped")
        gated = sem("gated")
        out_projected = sem("out_projected")
        mixed_done = sem("mixed_done")
        scattered = sem("scattered")
        added = sem("added")

        LOADS = 8
        block = ctx.enter_context(nc.Block())

        @block.sync
        def _(sp):
            for dst, src in ((conv_w[:, :, :], w["conv_w"].rearrange("(c p) k -> p c k", p=P)),
                             (conv_b[:, :], w["conv_b"]),
                             (xproj_w[:, :, :], w["xproj_w"].rearrange("(c p) k -> p c k", p=P)),
                             (dt_w[:, :], w["dt_w"]),
                             (dt_b[:, :], w["dt_b"]),
                             (a_log[:, :, :], w["A_log"].rearrange("(c p) k -> p c k", p=P)),
                             (skip[:, :], w["Dp"]),
                             (out_w[:, :, :], w["out_w"].rearrange("(c p) k -> p c k", p=P))):
                sp.dma_start(dst, src).then_inc(loaded, 16)

        @block.gpsimd
        def _(pool):
            pool.memset(parts[:, :].bitcast(F32), 0.0).then_inc(blank, 1)
            pool.memset(pick[:, :].bitcast(F32), 0.0).then_inc(blank, 1)
            for i in range(DECAYS):
                pool.memset(decay[i][:, :, 0:1], 0.0).then_inc(zeroed, 1)
            for ct in range(CT):
                pool.wait_ge(delta_done, ct + 1)
                pool.tensor_tensor(dx[:, ct, :], delta[:, ct, :], xc[:, ct, :], ALU.mult).then_inc(dx_done, 1)
            pool.wait_ge(dx_done, CT)
            for n in range(CT * DS):
                ct, s = n // DS, n % DS
                if ct == 0:
                    pool.wait_ge((bc_stored_a, bc_stored_v)[s % 2], s // 2 + 1)
                if n >= RINGS:
                    pool.wait_ge(summed, n - RINGS + 1)
                pool.tensor_tensor(drive[n % RINGS][:, :], dx[:, ct, :], bc[:, s, :], ALU.mult).then_inc(drive_done, 1)

        @block.scalar
        def _(act):
            for ct in range(CT):
                act.wait_ge(conv_done, ct + 1)
                nc.scalar.activation(delta[:, ct, :], xc[:, ct, :], ACT.Tanh, scale=0.5).then_inc(conv_tanh, 1)
            act.wait_ge(loaded, 16 * LOADS)
            nc.scalar.activation(a_neg[:, :, :], a_log[:, :, :], ACT.Exp).then_inc(a_exp, 1)
            act.wait_ge(projected, 1)
            for h in range(2):
                nc.scalar.activation(proj[:, h * HT:(h + 1) * HT], banks[h][0:RANK, 0:HT],
                                     ACT.Copy).then_inc(proj_stored, 1)
            act.wait_ge(blank, 2)
            for h in range(2):
                nc.scalar.activation(parts[0:RANK, h * HT:(h + 1) * HT], banks[h][0:RANK, 0:HT],
                                     ACT.Copy).then_inc(proj_hi_done, 1)
            for ct in range(CT):
                for h in range(2):
                    at = slice(h * HT, (h + 1) * HT)
                    act.wait_ge(dt_projected, 2 * ct + h + 1)
                    nc.scalar.activation(delta[:, ct, at], banks[2 + (2 * ct + h) % 4][:, 0:HT], ACT.Identity,
                                         bias=dt_b[:, ct:ct + 1]).then_inc(dt_biased, 1)
                act.wait_ge(dt_biased, 2 * ct + 2)
                if ct >= 2:
                    act.wait_ge(delta_done, ct - 1)
                part = drive[ct % 2][:, :]
                nc.scalar.activation(part, delta[:, ct, :], ACT.Abs).then_inc(soft, 1)
                act.wait_ge(soft, 3 * ct + 1)
                nc.scalar.activation(part, part, ACT.Exp, scale=-1.0).then_inc(soft, 1)
                act.wait_ge(soft, 3 * ct + 2)
                nc.scalar.activation(part, part, ACT.Ln, bias=1.0).then_inc(soft, 1)
            for r in range(0, 2 * DS, 2):
                for h in range(2):
                    act.wait_ge(spread, 2 * r + h + 1)
                    i = nc.scalar.activation(bc[:, r, h * HT:(h + 1) * HT], banks[2 * (r % 4) + h][:, 0:HT],
                                             ACT.Copy)
                i.then_inc(bc_stored_a, 1)
            act.wait_ge(a_ready, 1)
            act.wait_ge(delta_done, CT)
            act.wait_ge(zeroed, DECAYS)
            for n in range(CT * DS):
                ct, s = n // DS, n % DS
                if n >= DECAYS:
                    act.wait_ge(scanned, n - DECAYS + 1)
                nc.scalar.activation(decay[n % DECAYS][:, :, 1:NS],
                                     delta[:, ct, :].rearrange("p (b t) -> p b t", b=B)[:, :, 1:NS], ACT.Exp,
                                     scale=a_neg[:, ct, s:s + 1]).then_inc(decay_done, 1)

        @block.vector
        def _(dve):
            dve.wait_ge(loaded, 16 * LOADS)
            step = 0
            for ct in range(CT):
                out = xc[:, ct, :].rearrange("p (b t) -> p b t", b=B)
                dve.tensor_scalar(out, xi[:, ct, :, 0:NS], conv_w[:, ct, 0:1], conv_b[:, ct:ct + 1],
                                  ALU.mult, ALU.add).then_inc(half_done, 1)
                for j in range(1, DCONV):
                    step += 1
                    dve.wait_ge(half_done, step)
                    dve.scalar_tensor_tensor(out, xi[:, ct, :, j:j + NS], conv_w[:, ct, j:j + 1], out,
                                             ALU.mult, ALU.add).then_inc(
                                                 half_done if j < DCONV - 1 else conv_done, 1)
            for ct in range(CT):
                dve.wait_ge(conv_tanh, ct + 1)
                dve.tensor_scalar(delta[:, ct, :], delta[:, ct, :], 0.5, 0.5, ALU.mult, ALU.add).then_inc(half_done, 1)
                step += 1
                dve.wait_ge(half_done, step)
                dve.tensor_tensor(xc[:, ct, :], xc[:, ct, :], delta[:, ct, :], ALU.mult).then_inc(xc_done, 1)
            dve.wait_ge(blank, 2)
            for at in (0, LOW):
                dve.tensor_copy(pick[at:at + RANK, :], ident[0:RANK, 0:RANK]).then_inc(pick_ready, 1)
            dve.wait_ge(a_exp, 1)
            dve.tensor_scalar(a_neg[:, :, :], a_neg[:, :, :], -1.0, None, ALU.mult).then_inc(a_ready, 1)
            dve.wait_ge(proj_stored, 2)
            dve.wait_ge(proj_hi_done, 2)
            dve.tensor_tensor(parts[LOW:LOW + RANK, :], proj[:, :], parts[0:RANK, :].bitcast(F32),
                              ALU.subtract).then_inc(proj_split, 1)
            for ct in range(CT):
                dve.wait_ge(soft, 3 * ct + 3)
                dve.scalar_tensor_tensor(delta[:, ct, :], delta[:, ct, :], 0.0, drive[ct % 2][:, :],
                                         ALU.max, ALU.add).then_inc(delta_done, 1)
            for r in range(1, 2 * DS, 2):
                for h in range(2):
                    dve.wait_ge(spread, 2 * r + h + 1)
                    i = dve.tensor_copy(bc[:, r, h * HT:(h + 1) * HT], banks[2 * (r % 4) + h][:, 0:HT])
                i.then_inc(bc_stored_v, 1)
            dve.wait_ge(bc_stored_a, DS)
            dve.wait_ge(bc_stored_v, DS)

            def finish(ct):
                dve.wait_ge(summed, DS * (ct + 1))
                for h in range(2):
                    at = slice(h * HT, (h + 1) * HT)
                    dve.scalar_tensor_tensor(xc[:, ct, at], xc[:, ct, at], skip[:, ct:ct + 1],
                                             banks[2 * (ct % 2) + h][:, 0:HT], ALU.mult, ALU.add).then_inc(skipped, 1)
                dve.wait_ge(skipped, 2 * ct + 2)
                dve.scalar_tensor_tensor(xc[:, ct, :], xc[:, ct, :], 0.5,
                                         z_gate[:, ct, :, :].rearrange("p b t -> p (b t)"),
                                         ALU.mult, ALU.mult).then_inc(gated, 1)

            for n in range(CT * DS):
                ct, s = n // DS, n % DS
                dve.wait_ge(decay_done, n + 1)
                dve.wait_ge(drive_done, n + 1)
                dve.tensor_tensor_scan(drive[n % RINGS][:, :], decay[n % DECAYS][:, :, :].rearrange("p b t -> p (b t)"),
                                       drive[n % RINGS][:, :], 0.0, ALU.mult, ALU.add).then_inc(scanned, 1)
                dve.wait_ge(scanned, n + 1)
                dve.tensor_tensor(drive[n % RINGS][:, :], drive[n % RINGS][:, :], bc[:, DS + s, :],
                                  ALU.mult).then_inc(read_out, 1)
                if s == 2 and ct > 0:
                    finish(ct - 1)
            finish(CT - 1)
            for b in range(B):
                dve.wait_ge(out_projected, 2 * b + 1)
                dve.tensor_copy(mixed[:, b, 0, :], banks[4 + 2 * (b % 2)][:, 0:D]).then_inc(mixed_done, 1)
                dve.wait_ge(out_projected, 2 * b + 2)
                dve.tensor_copy(mixed[0:NS - P, b, 1, :], banks[5 + 2 * (b % 2)][0:NS - P, 0:D]).then_inc(mixed_done, 1)
            for t in range(TT):
                dve.wait_ge(scattered, t + 1)
                dve.tensor_tensor(X1[:, t, :], X1[:, t, :], banks[t % 4][:, 0:D], ALU.add).then_inc(added, 1)

        @block.tensor
        def _(pe):
            pe.wait_ge(loaded, 16 * LOADS)
            for ct in range(CT):
                pe.wait_ge(xc_done, ct + 1)
                for h in range(2):
                    i = pe.matmul(banks[h][0:RANK, 0:HT], xproj_w[:, ct, :], xc[:, ct, h * HT:(h + 1) * HT],
                                  start=(ct == 0), stop=(ct == CT - 1))
            i.then_inc(projected, 1)
            pe.wait_ge(proj_stored, 2)
            for ct in range(CT):
                for h in range(2):
                    n = 2 * ct + h
                    if n >= 4:
                        pe.wait_ge(dt_biased, n - 3)
                    pe.matmul(banks[2 + n % 4][:, 0:HT], dt_w[:, ct * P:(ct + 1) * P],
                              proj[0:DTR, h * HT:(h + 1) * HT], start=True, stop=True).then_inc(dt_projected, 1)
            pe.wait_ge(dt_biased, 2 * CT)
            pe.wait_ge(pick_ready, 2)
            pe.wait_ge(proj_split, 1)
            for r in range(2 * DS):
                if r >= 4:
                    pe.wait_ge((bc_stored_a, bc_stored_v)[r % 2], (r - 4) // 2 + 1)
                for h in range(2):
                    pe.matmul(banks[2 * (r % 4) + h][:, 0:HT],
                              pick[:, DTR + r:DTR + r + 1].broadcast_to([P, P]),
                              parts[:, h * HT:(h + 1) * HT], start=True, stop=True).then_inc(spread, 1)
            pe.wait_ge(bc_stored_a, DS)
            pe.wait_ge(bc_stored_v, DS)
            for n in range(CT * DS):
                ct, s = n // DS, n % DS
                if s == 0 and ct >= 2:
                    pe.wait_ge(gated, ct - 1)
                pe.wait_ge(read_out, n + 1)
                for h in range(2):
                    i = pe.matmul(banks[2 * (ct % 2) + h][:, 0:HT], ident[:, :],
                                  drive[n % RINGS][:, h * HT:(h + 1) * HT], start=(s == 0), stop=(s == DS - 1))
                i.then_inc(summed, 1)
            pe.wait_ge(gated, CT)
            for b in range(B):
                for a in range(2):
                    if b >= 2:
                        pe.wait_ge(mixed_done, 2 * (b - 2) + a + 1)
                    m = P if a == 0 else NS - P
                    for ct in range(CT):
                        i = pe.matmul(banks[4 + 2 * (b % 2) + a][0:m, 0:D],
                                      xc[:, ct, b * NS + a * P:b * NS + a * P + m], out_w[:, ct, :],
                                      start=(ct == 0), stop=(ct == CT - 1))
                    i.then_inc(out_projected, 1)
            for t in range(TT):
                b = t // QT
                pe.wait_ge(mixed_done, 2 * b + 2)
                if t >= 4:
                    pe.wait_ge(added, t - 3)
                for a in range(2):
                    i = pe.matmul(banks[t % 4][:, 0:D], perm_T[:, b, a, (t % QT) * P:(t % QT + 1) * P],
                                  mixed[:, b, a, :], start=(a == 0), stop=(a == 1))
                i.then_inc(scattered, 1)


def experts(nc, w, X1, out, ident, banks):
    ctx = ExitStack()
    with ctx:
        def sb(name, shape, dt=F32):
            return ctx.enter_context(nc.sbuf_tensor(f"ex_{name}", shape, dt))

        def sem(name):
            return ctx.enter_context(nc.semaphore(f"ex_{name}"))

        NTOK = B * N1
        HALF = NTOK // 2
        router = sb("router", [P, DC, E])
        raw = sb("raw", [P, 3, DC, HID])
        w_hi = [sb(f"w_hi{i}", [P, 3, DC, HID], F32R) for i in range(2)]
        w_lo = [sb(f"w_lo{i}", [P, 3, DC, HID], F32R) for i in range(2)]
        less = sb("less", [P, E, E])
        xf = sb("xf", [P, TT, D])
        xf_T = sb("xf_T", [P, DC, NTOK])
        x_hi = sb("x_hi", [P, DC, NTOK], F32R)
        x_lo = sb("x_lo", [P, DC, NTOK], F32R)
        logits = sb("logits", [P, TT, E])
        top = sb("top", [P, TT])
        p = sb("p", [P, TT, E])
        same = sb("same", [P, TT, E, E])
        above = sb("above", [P, TT, E, E])
        rank = sb("rank", [P, TT, E])
        chosen = sb("chosen", [P, TT, E])
        csum = sb("csum", [P, TT])
        combine = sb("combine", [P, TT, E])
        tanh = sb("tanh", [P, 2, HALF])
        gated = sb("gated", [P, 2, HALF])
        hidden = sb("hidden", [P, 2, HALF])
        h_hi = sb("h_hi", [P, HC2, NTOK], F32R)
        h_lo = sb("h_lo", [P, HC2, NTOK], F32R)
        norm = Norm(sb, sem, "norm", TT)

        router_loaded = sem("router_loaded")
        up_loaded = sem("up_loaded")
        down_loaded = sem("down_loaded")
        consts = sem("consts")
        masked = sem("masked")
        up_hi_done = sem("up_hi_done")
        up_split = sem("up_split")
        down_hi_done = sem("down_hi_done")
        down_split = sem("down_split")
        transposed = sem("transposed")
        xf_T_stored = sem("xf_T_stored")
        x_hi_done = sem("x_hi_done")
        x_split = sem("x_split")
        logits_ready = sem("logits_ready")
        step = sem("step")
        p_exp = sem("p_exp")
        combine_ready = sem("combine_ready")
        gate_ready = sem("gate_ready")
        tanh_done = sem("tanh_done")
        gated_done = sem("gated_done")
        hidden_done = sem("hidden_done")
        h_hi_done = sem("h_hi_done")
        h_split = sem("h_split")
        down_done = [sem(f"down_done{half}") for half in range(2)]
        added = sem("added")
        stored = sem("stored")

        TH = TT // 2
        BUFFERS = 2
        GU = 2 * HC2
        block = ctx.enter_context(nc.Block())

        @block.sync
        def _(sp):
            sp.dma_start(router[:, :, :], w["router_w"].rearrange("(c p) e -> p c e", p=P)).then_inc(router_loaded, 16)

            def load_up(e):
                for kind, name in enumerate(("w_gate", "w_up")):
                    sp.dma_start(raw[:, kind, :, :], w[name][bass.ds(e, 1), :, :].rearrange(
                        "o (c p) h -> p (o c) h", p=P)).then_inc(up_loaded, 16)

            def load_down(e):
                sp.dma_start(raw[:, 2, :, :].rearrange("p a n -> p (a n)").rearrange("p (c d) -> p c d", d=D),
                             w["w_down"][bass.ds(e, 1), :, :].rearrange(
                                 "o (c p) d -> p (o c) d", p=P)).then_inc(down_loaded, 16)

            load_up(0)
            load_down(0)
            with sp.Fori(1, E) as e:
                sp.wait_ge(up_split, e)
                load_up(e)
                sp.wait_ge(down_split, e)
                load_down(e)
            y = out.rearrange("b (t p) d -> p (b t) d", p=P)
            for half in range(2):
                tiles = slice(half * TH, (half + 1) * TH)
                sp.wait_ge(added, (E - 1) * TT + (half + 1) * TH + OPEN)
                sp.dma_start(y[:, tiles, :], X1[:, tiles, :]).then_inc(stored, 16)
            sp.wait_ge(stored, 32)

        @block.gpsimd
        def _(pool):
            pool.memset(less[:, :, :], 1.0).then_inc(consts, 1)
            pool.wait_ge(consts, 1)
            pool.affine_select(out=less[:, :, :], in_=less[:, :, :], compare_op=ALU.is_gt, fill=0.0,
                               base=0, pattern=[[1, E], [-1, E]], channel_multiplier=0).then_inc(masked, 1)

            def up_low(i, e):
                pool.wait_ge(up_hi_done, e + 1)
                pool.tensor_tensor(w_lo[i][:, 0:2, :, :], raw[:, 0:2, :, :], w_hi[i][:, 0:2, :, :].bitcast(F32),
                                   ALU.subtract).then_inc(up_split, 1)

            def down_low(i, e):
                pool.wait_ge(down_hi_done, e + 1)
                pool.tensor_tensor(w_lo[i][:, 2, :, :], raw[:, 2, :, :], w_hi[i][:, 2, :, :].bitcast(F32),
                                   ALU.subtract).then_inc(down_split, 1)

            def low_parts(e, half):
                pool.wait_ge(down_done[half], e * TH + OPEN)
                for c in range(HC2):
                    n = half * HC2 + c
                    at = slice(half * HALF, (half + 1) * HALF)
                    pool.wait_ge(h_hi_done, e * GU + n + 1)
                    pool.tensor_tensor(h_lo[:, c, at], hidden[:, n % 2, :], h_hi[:, c, at].bitcast(F32),
                                       ALU.subtract).then_inc(h_split, 1)

            def expert(e, k, up_next, down_next):
                low_parts(e, 0)
                if down_next:
                    down_low(1 - k, e + 1)
                low_parts(e, 1)
                if up_next:
                    up_low(k, e + 2)

            pool.sem_inc(h_split, BUFFERS)
            up_low(0, 0)
            down_low(0, 0)
            up_low(1, 1)
            with pool.Fori(0, E // 2 - 1) as i:
                for k in range(2):
                    expert(2 * i + k, k, True, True)
            expert(E - 2, 0, False, True)
            expert(E - 1, 1, False, False)

        @block.scalar
        def _(act):
            act.wait_ge(up_loaded, 32)
            nc.scalar.activation(w_hi[0][:, 0:2, :, :], raw[:, 0:2, :, :], ACT.Copy).then_inc(up_hi_done, 1)
            act.wait_ge(down_loaded, 16)
            nc.scalar.activation(w_hi[0][:, 2, :, :], raw[:, 2, :, :], ACT.Copy).then_inc(down_hi_done, 1)
            norm.root(act, 0)
            for t in range(TT):
                act.wait_ge(transposed, t + 1)
                nc.scalar.activation(xf_T[:, :, t * P:(t + 1) * P],
                                     banks[t][:, 0:DC * P].rearrange("p (c q) -> p c q", c=DC),
                                     ACT.Copy).then_inc(xf_T_stored, 1)
            act.wait_ge(up_loaded, 64)
            nc.scalar.activation(w_hi[1][:, 0:2, :, :], raw[:, 0:2, :, :], ACT.Copy).then_inc(up_hi_done, 1)
            act.wait_ge(step, 2)
            nc.scalar.activation(p[:, :, :], logits[:, :, :], ACT.Exp).then_inc(p_exp, 1)

            def up_high(i, e):
                act.wait_ge(up_loaded, e * 32 + 32)
                nc.scalar.activation(w_hi[i][:, 0:2, :, :], raw[:, 0:2, :, :], ACT.Copy).then_inc(up_hi_done, 1)

            def down_high(i, e):
                act.wait_ge(down_loaded, e * 16 + 16)
                nc.scalar.activation(w_hi[i][:, 2, :, :], raw[:, 2, :, :], ACT.Copy).then_inc(down_hi_done, 1)

            def expert(e, k, up_next, down_next):
                for n in range(GU):
                    half, c = n // HC2, n % HC2
                    at = slice(half * HALF, (half + 1) * HALF)
                    act.wait_ge(gate_ready, e * GU + n + 1)
                    act.wait_ge(gated_done, e * GU + n - 1 + BUFFERS)
                    nc.scalar.activation(tanh[:, n % 2, :], banks[2 * (n % 2)][:, :], ACT.Tanh,
                                         scale=0.5).then_inc(tanh_done, 1)
                    if c == 0:
                        act.wait_ge(down_done[half], e * TH + OPEN)
                    act.wait_ge(hidden_done, e * GU + n + 1 + BUFFERS)
                    nc.scalar.activation(h_hi[:, c, at], hidden[:, n % 2, :], ACT.Copy).then_inc(h_hi_done, 1)
                    if down_next and n == HC2 - 1:
                        act.wait_ge(down_done[1], e * TH + OPEN)
                        down_high(1 - k, e + 1)
                if up_next:
                    up_high(k, e + 2)

            with act.Fori(0, E // 2 - 1) as i:
                for k in range(2):
                    expert(2 * i + k, k, True, True)
            expert(E - 2, 0, False, True)
            expert(E - 1, 1, False, False)

        @block.vector
        def _(dve):
            dve.sem_inc(added, OPEN)
            for opened in (gated_done, hidden_done):
                dve.sem_inc(opened, BUFFERS)
            norm.normalize(dve, 0, X1, xf)
            for t in range(TT):
                at = slice(t * P, (t + 1) * P)
                dve.wait_ge(xf_T_stored, t + 1)
                dve.tensor_copy(x_hi[:, :, at], xf_T[:, :, at]).then_inc(x_hi_done, 1)
                dve.wait_ge(x_hi_done, t + 1)
                dve.tensor_tensor(x_lo[:, :, at], xf_T[:, :, at], x_hi[:, :, at].bitcast(F32),
                                  ALU.subtract).then_inc(x_split, 1)
            dve.wait_ge(logits_ready, 1)
            scores = banks[7][:, 0:TT * E].rearrange("p (t e) -> p t e", t=TT)
            dve.tensor_reduce(top[:, :], scores, AX_X, ALU.max).then_inc(step, 1)
            dve.wait_ge(step, 1)
            dve.tensor_tensor(logits[:, :, :], scores, top[:, :].unsqueeze(2).broadcast_to([P, TT, E]),
                              ALU.subtract).then_inc(step, 1)
            dve.wait_ge(p_exp, 1)
            dve.wait_ge(masked, 1)
            of_f = p[:, :, :].unsqueeze(2).broadcast_to([P, TT, E, E])
            of_e = p[:, :, :].unsqueeze(3).broadcast_to([P, TT, E, E])
            dve.tensor_tensor(same[:, :, :, :], of_f, of_e, ALU.is_equal).then_inc(step, 1)
            dve.tensor_tensor(above[:, :, :, :], of_f, of_e, ALU.is_gt).then_inc(step, 1)
            dve.wait_ge(step, 4)
            dve.tensor_tensor(same[:, :, :, :], same[:, :, :, :],
                              less[:, :, :].unsqueeze(1).broadcast_to([P, TT, E, E]), ALU.mult).then_inc(step, 1)
            dve.wait_ge(step, 5)
            dve.tensor_tensor(above[:, :, :, :], above[:, :, :, :], same[:, :, :, :], ALU.add).then_inc(step, 1)
            dve.wait_ge(step, 6)
            dve.tensor_reduce(rank[:, :, :], above[:, :, :, :], AX_X, ALU.add).then_inc(step, 1)
            dve.wait_ge(step, 7)
            dve.tensor_scalar(chosen[:, :, :], rank[:, :, :], float(K_TOP), None, ALU.is_lt).then_inc(step, 1)
            dve.wait_ge(step, 8)
            dve.tensor_tensor(chosen[:, :, :], chosen[:, :, :], p[:, :, :], ALU.mult).then_inc(step, 1)
            dve.wait_ge(step, 9)
            dve.tensor_reduce(csum[:, :], chosen[:, :, :], AX_X, ALU.add).then_inc(step, 1)
            dve.wait_ge(step, 10)
            dve.reciprocal(top[:, :], csum[:, :]).then_inc(step, 1)
            dve.wait_ge(step, 11)
            dve.scalar_tensor_tensor(combine[:, :, :], chosen[:, :, :], 0.5,
                                     top[:, :].unsqueeze(2).broadcast_to([P, TT, E]),
                                     ALU.mult, ALU.mult).then_inc(combine_ready, 1)
            dve.wait_ge(combine_ready, 1)

            def pieces(e, half):
                for c in range(HC2):
                    n = half * HC2 + c
                    b = 2 * (n % 2)
                    dve.wait_ge(tanh_done, e * GU + n + 1)
                    dve.scalar_tensor_tensor(gated[:, n % 2, :], tanh[:, n % 2, :], 1.0, banks[b][:, :],
                                             ALU.add, ALU.mult).then_inc(gated_done, 1)
                    dve.wait_ge(gated_done, e * GU + n + 1 + BUFFERS)
                    dve.wait_ge(h_split, e * GU + n - 1 + BUFFERS)
                    dve.tensor_tensor(hidden[:, n % 2, :], gated[:, n % 2, :], banks[b + 1][:, :],
                                      ALU.mult).then_inc(hidden_done, 1)

            def add(e, half):
                for t in range(half * TT // 2, (half + 1) * TT // 2):
                    dve.wait_ge(down_done[half], e * TH + t % TH + 1 + OPEN)
                    dve.scalar_tensor_tensor(X1[:, t, :], banks[4 + t % 4][:, 0:D],
                                             combine[:, t, bass.ds(e, 1)], X1[:, t, :],
                                             ALU.mult, ALU.add).then_inc(added, 1)

            pieces(0, 0)
            pieces(0, 1)
            add(0, 0)
            with dve.Fori(1, E) as e:
                pieces(e, 0)
                add(e - 1, 1)
                pieces(e, 1)
                add(e, 0)
            add(E - 1, 1)

        @block.tensor
        def _(pe):
            for opened in down_done:
                pe.sem_inc(opened, OPEN)
            for t in range(TT):
                pe.wait_ge(norm.done, norm.tiles_done(0, t + 1))
                for c in range(DC):
                    i = pe.transpose(banks[t][:, c * P:(c + 1) * P], xf[:, t, c * P:(c + 1) * P], ident[:, :])
                i.then_inc(transposed, 1)
            pe.wait_ge(router_loaded, 16)
            pe.wait_ge(xf_T_stored, TT)
            for t in range(TT):
                for c in range(DC):
                    i = pe.matmul(banks[7][:, t * E:(t + 1) * E], xf_T[:, c, t * P:(t + 1) * P],
                                  router[:, c, :], start=(c == 0), stop=(c == DC - 1))
            i.then_inc(logits_ready, 1)
            pe.wait_ge(x_split, TT)

            def up(k, e, half):
                for c in range(HC2):
                    n = half * HC2 + c
                    b = 2 * (n % 2)
                    at = slice(half * HALF, (half + 1) * HALF)
                    pe.wait_ge(hidden_done, e * GU + n - 1 + BUFFERS)
                    for kind in range(2):
                        for d in range(DC):
                            wh, wl = (x[k][:, kind, d, c * P:(c + 1) * P] for x in (w_hi, w_lo))
                            pe.matmul(banks[b + kind][:, :], wh, x_hi[:, d, at], start=(d == 0), stop=False)
                            pe.matmul(banks[b + kind][:, :], wh, x_lo[:, d, at], start=False, stop=False)
                            i = pe.matmul(banks[b + kind][:, :], wl, x_hi[:, d, at], start=False,
                                          stop=(d == DC - 1))
                    i.then_inc(gate_ready, 1)

            def down(k, e, half):
                for t in range(half * TT // 2, (half + 1) * TT // 2):
                    if t == half * TT // 2:
                        pe.wait_ge(h_split, e * GU + (half + 1) * HC2 + BUFFERS)
                    if t >= 4:
                        pe.wait_ge(added, e * TT + t - 3 + OPEN)
                    elif t == 0:
                        pe.wait_ge(added, e * TT + OPEN)
                    for c in range(HC2):
                        hh, hl = (x[:, c, t * P:(t + 1) * P] for x in (h_hi, h_lo))
                        wh, wl = (x[k][:, 2, :, :].rearrange("p a n -> p (a n)")[:, c * D:(c + 1) * D]
                                  for x in (w_hi, w_lo))
                        o = banks[4 + t % 4][:, 0:D]
                        pe.matmul(o, hh, wh, start=(c == 0), stop=False)
                        pe.matmul(o, hh, wl, start=False, stop=False)
                        i = pe.matmul(o, hl, wh, start=False, stop=(c == HC2 - 1))
                    i.then_inc(down_done[half], 1)

            def expert(e, k, up_next):
                up(k, e, 1)
                pe.wait_ge(down_split, e + 1)
                down(k, e, 0)
                if up_next:
                    pe.wait_ge(up_split, e + 2)
                    up(1 - k, e + 1, 0)
                down(k, e, 1)

            pe.wait_ge(up_split, 1)
            up(0, 0, 0)
            pe.wait_ge(combine_ready, 1)
            with pe.Fori(0, E // 2 - 1) as i:
                for k in range(2):
                    expert(2 * i + k, k, True)
            expert(E - 2, 0, True)
            expert(E - 1, 1, False)


def program(nc, x, ctxT, xattn, attn, ffn, out):
    ctx = ExitStack()
    with ctx:
        X1 = ctx.enter_context(nc.sbuf_tensor("X1", [P, TT, D], F32))
        ident = ctx.enter_context(nc.sbuf_tensor("ident", [P, P], F32))
        banks = [ctx.enter_context(nc.psum_tensor(f"bank{i}", [P, 512], F32)) for i in range(8)]
        cross_attention(nc, x, ctxT, xattn, X1, ident, banks)
        with ExitStack() as mixer:
            def sb(name, shape):
                return mixer.enter_context(nc.sbuf_tensor(name, shape, F32))

            perm_T = sb("perm_T", [P, B, 2, N1])
            mixed = sb("mixed", [P, B, 2, D])
            xi = sb("xi", [P, CT, B, NS + DCONV - 1])
            z_gate = sb("z_gate", [P, CT, B, NS])
            route_and_project(nc, attn, X1, perm_T, xi, z_gate, mixed, ident, banks)
            state_space(nc, attn, X1, perm_T, xi, z_gate, mixed, ident, banks)
        experts(nc, ffn, X1, out, ident, banks)


def kernel(**inputs):
    import concourse.bacc as _bacc
    from concourse.bass_utils import run_bass_kernel_spmd as _run

    nc = _bacc.Bacc("TRN2", target_bir_lowering=False, num_devices=1)
    arrays = {}

    def give(name, a):
        a = np.ascontiguousarray(a)
        arrays[f"in_{name}_dram"] = a
        return nc.dram_tensor(f"in_{name}_dram", a.shape, mybir.dt.from_np(a.dtype), kind="ExternalInput").ap()

    x = give("x", inputs["x"])
    ctxT = give("ctxT", np.asarray(inputs["ctx_1024"]).transpose(0, 2, 1))
    xattn, attn, ffn = {}, {}, {}
    for name, a in inputs.items():
        a = np.asarray(a)
        if name.startswith("L0_xattn_"):
            xattn[name[9:]] = give(name, a)
        elif name.startswith("L0_attn_"):
            if name[8:] in ("bq", "bk", "conv_b", "dt_b", "Dp"):
                a = a.reshape(-1, P).T
            attn[name[8:]] = give(name, a)
        elif name == "L0_ffn_router_w":
            ffn["router_w"] = give(name, a.T)
        elif name.startswith("L0_ffn_"):
            ffn[name[7:]] = give(name, a.transpose(0, 2, 1))
    out = nc.dram_tensor("out_0_dram", (B, N1, D), F32, kind="ExternalOutput").ap()
    program(nc, x, ctxT, xattn, attn, ffn, out)
    r = _run(nc, [arrays], core_ids=[0])
    return r.results[0]["out_0_dram"]
```
